# Optimizing a Trainium2 kernel written in Bass

```python
import numpy as np
import jax
import jax.numpy as jnp

def _softmax(x, axis=-1):
    return jax.nn.softmax(x, axis=axis)

def _gelu(x):
    return jax.nn.gelu(x, approximate=True)

def _silu(x):
    return jax.nn.silu(x)

def _sigmoid(x):
    return jax.nn.sigmoid(x)

def _layernorm(x, axis=-1, eps=1e-05):
    m = jnp.mean(x, axis=axis, keepdims=True)
    v = jnp.var(x, axis=axis, keepdims=True)
    return (x - m) / jnp.sqrt(v + eps)

def _scatter_add(tgt, idx, src, axis=0):
    return tgt.at[idx].add(src)

def _segment_sum(src, seg, n):
    return jax.ops.segment_sum(src, seg, n)
kernel_name = 'mk_conv_attn_hybrid_d2_conv_nchw256_r4_bcb2ce'

def setup_inputs(seed: int=0):
    np.random.seed(seed)
    _w = jnp.asarray

    def _rec_inputs():
        import jax
        import jax.numpy as jnp
        _gk = jax.random.key(seed)
        x = -0.0003929 + 0.9999 * jax.random.normal(jax.random.fold_in(_gk, 1), (16, 64, 16, 16), jnp.float32)
        return x
    x = _rec_inputs()

    def _L0_conv_setup():
        import jax, jax.numpy as jnp
        import numpy as np
        from jax import lax
        EPS = 1e-05
        RADIX, CARD = (2, 2)
        WS = (8, 8)
        NORM_G = 32

        def group_norm(x, groups):
            B, C, H, W = x.shape
            xr = x.reshape(B, groups, -1)
            mean = xr.mean(-1, keepdims=True)
            var = xr.var(-1, keepdims=True)
            xr = (xr - mean) * lax.rsqrt(var + EPS)
            return xr.reshape(B, C, H, W)

        def conv2d(x, w, b, padding=0, groups=1):
            out = lax.conv_general_dilated(x, w, (1, 1), ((padding, padding), (padding, padding)), feature_group_count=groups, dimension_numbers=('NCHW', 'OIHW', 'NCHW'))
            return out + b[None, :, None, None]
        key = jax.random.key(seed)
        ks = jax.random.split(key, 10)
        B, Cin, H, W = (16, 64, 16, 16)
        C = 64
        inter = max(C // 8, 32)
        d = {}
        d['hidden_state'] = jax.random.normal(ks[0], (B, Cin, H, W), jnp.float32)
        d['w0'] = jax.random.normal(ks[1], (C, Cin, 1, 1), jnp.float32) / np.sqrt(Cin)
        d['b0'] = jax.random.normal(ks[2], (C,), jnp.float32) * 0.01
        d['w1'] = jax.random.normal(ks[3], (C * RADIX, C // (RADIX * CARD), 3, 3), jnp.float32) / np.sqrt(9 * C // (RADIX * CARD))
        d['b1'] = jax.random.normal(ks[4], (C * RADIX,), jnp.float32) * 0.01
        d['w2'] = jax.random.normal(ks[5], (inter * CARD, C // CARD, 1, 1), jnp.float32) / np.sqrt(C // CARD)
        d['b2'] = jax.random.normal(ks[6], (inter * CARD,), jnp.float32) * 0.01
        d['w3'] = jax.random.normal(ks[7], (C * RADIX, inter * CARD // CARD, 1, 1), jnp.float32) / np.sqrt(inter) / np.sqrt(C / CARD / RADIX)
        d['b3'] = jnp.zeros((C * RADIX,), jnp.float32)
        d['weight'] = jax.random.normal(ks[8], (C, C), jnp.float32) / np.sqrt(C)
        return d
    _L0_conv_all = _L0_conv_setup()
    _L0_conv_in = {k: v for k, v in _L0_conv_all.items() if k in ('w0', 'b0', 'w1', 'b1', 'w2', 'b2', 'w3', 'b3', 'weight')}
    del _L0_conv_all

    def _L1_attn_setup():
        import jax, jax.numpy as jnp
        import numpy as np
        T, N, D = (128, 256, 64)

        def _causal_attend(H, e):
            n = H.shape[1]
            m0 = jnp.full((n,), -jnp.inf, dtype=H.dtype)
            s0 = jnp.zeros((n,), dtype=H.dtype)
            num0 = jnp.zeros((n, H.shape[2]), dtype=H.dtype)

            def step(carry, inp):
                m, s, num = carry
                e_t, h_t = inp
                m_new = jnp.maximum(m, e_t)
                alpha = jnp.exp(m - m_new)
                p = jnp.exp(e_t - m_new)
                s_new = s * alpha + p
                num_new = num * alpha[:, None] + p[:, None] * h_t
                c_t = num_new / s_new[:, None]
                return ((m_new, s_new, num_new), c_t)
            _, C = jax.lax.scan(step, (m0, s0, num0), (e, H))
            return C
        key = jax.random.key(seed)
        k1, k2, k3, k4 = jax.random.split(key, 4)
        scale = 1.0 / np.sqrt(D)
        return {'H': jax.random.normal(k1, (T, N, D), dtype=jnp.float32), 'fc_w': jax.random.normal(k2, (D, D), dtype=jnp.float32) * scale, 'fc_b': jax.random.normal(k3, (D,), dtype=jnp.float32) * scale, 'score_w': jax.random.normal(k4, (D,), dtype=jnp.float32) * scale}
    _L1_attn_all = _L1_attn_setup()
    _L1_attn_in = {k: v for k, v in _L1_attn_all.items() if k in ('fc_w', 'fc_b', 'score_w')}
    del _L1_attn_all

    def _L1_ffn_setup():
        import jax, jax.numpy as jnp
        import numpy as np
        BN_EPS = 0.001

        def _bn(h, g, b, m, v):
            return g * (h - m) * jax.lax.rsqrt(v + BN_EPS) + b
        key = jax.random.key(seed)
        ks = jax.random.split(key, 8)
        B, F, Df = (64, 16, 64)
        E, H, D = (8, 64, 64)
        s1 = 1.0 / np.sqrt(Df)
        s2 = 1.0 / np.sqrt(H)
        return {'x': jax.random.normal(ks[0], (B, F, Df), jnp.float32), 'Wr': jax.random.normal(ks[1], (Df, E), jnp.float32) * s1, 'br': jnp.zeros((E,), jnp.float32), 'W1': jax.random.normal(ks[2], (E, Df, H), jnp.float32) * s1, 'b1': jnp.zeros((E, H), jnp.float32), 'g1': jnp.ones((E, H), jnp.float32), 'be1': jnp.zeros((E, H), jnp.float32), 'm1': jnp.zeros((E, H), jnp.float32), 'v1': jnp.ones((E, H), jnp.float32), 'W2': jax.random.normal(ks[3], (E, H, H), jnp.float32) * s2, 'b2': jnp.zeros((E, H), jnp.float32), 'g2': jnp.ones((E, H), jnp.float32), 'be2': jnp.zeros((E, H), jnp.float32), 'm2': jnp.zeros((E, H), jnp.float32), 'v2': jnp.ones((E, H), jnp.float32), 'Wo': jax.random.normal(ks[4], (E, H, D), jnp.float32) * s2, 'bo': jnp.zeros((E, D), jnp.float32)}
    _L1_ffn_all = _L1_ffn_setup()
    _L1_ffn_in = {k: v for k, v in _L1_ffn_all.items() if k in ('Wr', 'br', 'W1', 'b1', 'g1', 'be1', 'm1', 'v1', 'W2', 'b2', 'g2', 'be2', 'm2', 'v2', 'Wo', 'bo')}
    del _L1_ffn_all
    return {'x': x, 'L0_conv_w0': _L0_conv_in['w0'], 'L0_conv_b0': _L0_conv_in['b0'], 'L0_conv_w1': _L0_conv_in['w1'], 'L0_conv_b1': _L0_conv_in['b1'], 'L0_conv_w2': _L0_conv_in['w2'], 'L0_conv_b2': _L0_conv_in['b2'], 'L0_conv_w3': _L0_conv_in['w3'], 'L0_conv_b3': _L0_conv_in['b3'], 'L0_conv_weight': _L0_conv_in['weight'], 'L1_attn_fc_w': _L1_attn_in['fc_w'], 'L1_attn_fc_b': _L1_attn_in['fc_b'], 'L1_attn_score_w': _L1_attn_in['score_w'], 'L1_ffn_Wr': _L1_ffn_in['Wr'], 'L1_ffn_br': _L1_ffn_in['br'], 'L1_ffn_W1': _L1_ffn_in['W1'], 'L1_ffn_b1': _L1_ffn_in['b1'], 'L1_ffn_g1': _L1_ffn_in['g1'], 'L1_ffn_be1': _L1_ffn_in['be1'], 'L1_ffn_m1': _L1_ffn_in['m1'], 'L1_ffn_v1': _L1_ffn_in['v1'], 'L1_ffn_W2': _L1_ffn_in['W2'], 'L1_ffn_b2': _L1_ffn_in['b2'], 'L1_ffn_g2': _L1_ffn_in['g2'], 'L1_ffn_be2': _L1_ffn_in['be2'], 'L1_ffn_m2': _L1_ffn_in['m2'], 'L1_ffn_v2': _L1_ffn_in['v2'], 'L1_ffn_Wo': _L1_ffn_in['Wo'], 'L1_ffn_bo': _L1_ffn_in['bo']}

def reference(x, L0_conv_w0, L0_conv_b0, L0_conv_w1, L0_conv_b1, L0_conv_w2, L0_conv_b2, L0_conv_w3, L0_conv_b3, L0_conv_weight, L1_attn_fc_w, L1_attn_fc_b, L1_attn_score_w, L1_ffn_Wr, L1_ffn_br, L1_ffn_W1, L1_ffn_b1, L1_ffn_g1, L1_ffn_be1, L1_ffn_m1, L1_ffn_v1, L1_ffn_W2, L1_ffn_b2, L1_ffn_g2, L1_ffn_be2, L1_ffn_m2, L1_ffn_v2, L1_ffn_Wo, L1_ffn_bo):
    import jax
    import jax.numpy as jnp

    def _L0_conv_ref(hidden_state, w0, b0, w1, b1, w2, b2, w3, b3, weight):
        import jax, jax.numpy as jnp
        import numpy as np
        from jax import lax
        EPS = 1e-05
        RADIX, CARD = (2, 2)
        WS = (8, 8)
        NORM_G = 32

        def group_norm(x, groups):
            B, C, H, W = x.shape
            xr = x.reshape(B, groups, -1)
            mean = xr.mean(-1, keepdims=True)
            var = xr.var(-1, keepdims=True)
            xr = (xr - mean) * lax.rsqrt(var + EPS)
            return xr.reshape(B, C, H, W)

        def conv2d(x, w, b, padding=0, groups=1):
            out = lax.conv_general_dilated(x, w, (1, 1), ((padding, padding), (padding, padding)), feature_group_count=groups, dimension_numbers=('NCHW', 'OIHW', 'NCHW'))
            return out + b[None, :, None, None]
        B, Cin, H, W = hidden_state.shape
        x = group_norm(hidden_state, NORM_G)
        x = jax.nn.silu(conv2d(x, w0, b0))
        x = group_norm(x, RADIX * CARD * 4)
        x = jax.nn.silu(conv2d(x, w1, b1, padding=1, groups=RADIX * CARD))
        x = group_norm(x, CARD)
        C = x.shape[1] // RADIX
        Hn, Wn = (H // WS[0], W // WS[1])
        y = x.reshape(B, C, RADIX, Hn, WS[0], Wn, WS[1])
        a = y.mean(axis=(4, 6))
        a = a.max(axis=2)
        a = jax.nn.silu(conv2d(a, w2, b2, groups=CARD))
        a = group_norm(a, CARD * 4)
        a = conv2d(a, w3, b3, groups=CARD)
        a = a.reshape(B, C, RADIX, Hn, Wn)
        a = jax.nn.softmax(a, axis=2)
        out = jnp.einsum('BCRHhWw,BCRHW,Cc->BcHhWw', y, a, weight)
        out = out.reshape(B, C, H, W)
        out = group_norm(out, NORM_G)
        return hidden_state + out

    def _L1_attn_ref(H, fc_w, fc_b, score_w):
        import jax, jax.numpy as jnp
        import numpy as np
        T, N, D = (128, 256, 64)

        def _causal_attend(H, e):
            n = H.shape[1]
            m0 = jnp.full((n,), -jnp.inf, dtype=H.dtype)
            s0 = jnp.zeros((n,), dtype=H.dtype)
            num0 = jnp.zeros((n, H.shape[2]), dtype=H.dtype)

            def step(carry, inp):
                m, s, num = carry
                e_t, h_t = inp
                m_new = jnp.maximum(m, e_t)
                alpha = jnp.exp(m - m_new)
                p = jnp.exp(e_t - m_new)
                s_new = s * alpha + p
                num_new = num * alpha[:, None] + p[:, None] * h_t
                c_t = num_new / s_new[:, None]
                return ((m_new, s_new, num_new), c_t)
            _, C = jax.lax.scan(step, (m0, s0, num0), (e, H))
            return C
        Q = jnp.tanh(jnp.einsum('tnd,ed->tne', H, fc_w) + fc_b)
        e = jnp.einsum('tne,e->tn', Q, score_w)
        return _causal_attend(H, e)

    def _L1_ffn_ref(x, Wr, br, W1, b1, g1, be1, m1, v1, W2, b2, g2, be2, m2, v2, Wo, bo):
        import jax, jax.numpy as jnp
        import numpy as np
        BN_EPS = 0.001

        def _bn(h, g, b, m, v):
            return g * (h - m) * jax.lax.rsqrt(v + BN_EPS) + b
        feat = jnp.mean(x, axis=0)
        w = jax.nn.softmax(feat @ Wr + br, axis=-1)
        h = jnp.einsum('bfd,edh->bfeh', x, W1) + b1
        h = jax.nn.relu(_bn(h, g1, be1, m1, v1))
        h = jnp.einsum('bfeh,ehk->bfek', h, W2) + b2
        h = jax.nn.relu(_bn(h, g2, be2, m2, v2))
        y = jnp.einsum('bfeh,ehd->bfed', h, Wo) + bo
        return jnp.einsum('bfed,fe->bfd', y, w)

    def _gn(v, G=32, eps=1e-05):
        B_, C_, H_, W_ = v.shape
        g = v.reshape(B_, G, C_ // G, H_, W_)
        m = jnp.mean(g, axis=(2, 3, 4), keepdims=True)
        s = jnp.var(g, axis=(2, 3, 4), keepdims=True)
        return ((g - m) / jnp.sqrt(s + eps)).reshape(v.shape)

    def _ln_c(v, eps=1e-06):
        m = jnp.mean(v, axis=1, keepdims=True)
        s = jnp.var(v, axis=1, keepdims=True)
        return (v - m) / jnp.sqrt(s + eps)

    def _ln_t(v, eps=1e-05):
        m = jnp.mean(v, axis=-1, keepdims=True)
        s = jnp.var(v, axis=-1, keepdims=True)
        return (v - m) / jnp.sqrt(s + eps)

    def _to_tokens(v):
        B_, C_, H_, W_ = v.shape
        return v.reshape(B_, C_, H_ * W_).transpose(0, 2, 1)

    def _from_tokens(t, like):
        B_, C_, H_, W_ = like.shape
        return t.transpose(0, 2, 1).reshape(B_, C_, H_, W_)
    x = _L0_conv_ref(x, L0_conv_w0, L0_conv_b0, L0_conv_w1, L0_conv_b1, L0_conv_w2, L0_conv_b2, L0_conv_w3, L0_conv_b3, L0_conv_weight)
    t = _to_tokens(x)
    t = t + _L1_attn_ref(_ln_t(t), L1_attn_fc_w, L1_attn_fc_b, L1_attn_score_w)
    t = t + _L1_ffn_ref(_ln_t(t), L1_ffn_Wr, L1_ffn_br, L1_ffn_W1, L1_ffn_b1, L1_ffn_g1, L1_ffn_be1, L1_ffn_m1, L1_ffn_v1, L1_ffn_W2, L1_ffn_b2, L1_ffn_g2, L1_ffn_be2, L1_ffn_m2, L1_ffn_v2, L1_ffn_Wo, L1_ffn_bo)
    x = _from_tokens(t, x)
    return x

_drawn_inputs = setup_inputs


def setup_inputs(seed=0):
    import zlib

    import numpy as np

    out = dict(_drawn_inputs(seed))
    spreads = {'L0_conv_b3': (0.0, 0.1),
     'L1_ffn_br': (0.0, 0.8),
     'L1_ffn_b1': (0.0, 0.681),
     'L1_ffn_g1': (1.0, 0.6),
     'L1_ffn_be1': (0.0, 0.636),
     'L1_ffn_m1': (0.0, 0.673),
     'L1_ffn_v1': (1.0, 0.6),
     'L1_ffn_b2': (0.0, 0.44),
     'L1_ffn_g2': (1.0, 0.587),
     'L1_ffn_be2': (0.0, 0.518),
     'L1_ffn_m2': (0.0, 0.464),
     'L1_ffn_v2': (1.0, 0.6),
     'L1_ffn_bo': (0.0, 0.33)}
    factors = {'L0_conv_b0': 5.38, 'L0_conv_b1': 4.439, 'L0_conv_b2': 4.648, 'L1_attn_fc_b': 6.083}
    for name, (base, spread) in spreads.items():
        noise = np.random.default_rng([zlib.crc32(name.encode()), seed]).standard_normal(out[name].shape)
        drawn = base * np.exp(spread * noise) if base else spread * noise
        out[name] = jnp.asarray(drawn.astype(out[name].dtype))
    for name, factor in factors.items():
        out[name] = (out[name] * factor).astype(out[name].dtype)
    return out
```

```python
from contextlib import ExitStack

import concourse.bass as bass
from concourse import mybir

ALU = mybir.AluOpType
ACT = mybir.ActivationFunctionType
F32 = mybir.dt.float32
F32R = mybir.dt.float32r
AX_X = mybir.AxisListType.X

P = 128
B, C, S = 16, 64, 16
PIX = S * S
PAIRS = B // 2
NK = 2
PK = PAIRS // NK
BK = B // NK
PAD = S + 2
TAPS = 9
WIN = 4
E, HID = 8, 64
EP = E // 2
Q = 2
EPS = 1e-5
BN_EPS = 1e-3
LOWEST = -3.0e38

COLS = dict(
    gn1=P, gn2=P, ident=P, w0=P, b0=1, gn3=P, gna=C, w2=C, b2=1, w3=2 * P, b3=2, weight=C,
    fc=P, fcb=1, score=2, b1=1, wr=E, br=E, ffn1=EP * P, ffn2=EP * P, ffo=EP * C,
    bn1=5 * EP, bn2=5 * EP, emask=EP * E, sel=EP * P, bo=C, ones=P,
)


def columns():
    at, out = 0, {}
    for name, n in COLS.items():
        out[name] = (at, at + n)
        at += n
    return out, at


def conv_attention_experts(nc: bass.Bass, x: bass.AP, params: bass.AP, conv1_w: bass.AP, out: bass.AP):
    where, n_params = columns()
    x_pairs = x.rearrange("(b h) c y x -> b (h c) (y x)", h=2)
    out_pairs = out.rearrange("(b h) c y x -> b (h c) (y x)", h=2)

    with ExitStack() as ctx:
        def sb(name, shape, dt=F32):
            return ctx.enter_context(nc.sbuf_tensor(name, shape, dt))

        def sem(name):
            return ctx.enter_context(nc.semaphore(name))

        par = sb("par", [P, n_params])

        def w(name, rows=P):
            a, b = where[name]
            return par[0:rows, a:b]

        xin = sb("xin", [P, PAIRS, PIX])
        xnorm = sb("xnorm", [P, PAIRS, PIX])
        act0 = sb("act0", [P, PAIRS, PIX])
        norm0 = sb("norm0", [P, PAIRS, PIX])
        pad = [sb(f"pad{h}", [P, PAIRS, PAD, PAD], F32R) for h in range(2)]
        y = sb("y", [P, B, PIX])
        x1 = sb("x1", [P, PAIRS, PIX])
        tok = sb("tok", [P, Q, B, C])
        square = sb("square", [P, Q, B, C])
        hn = sb("hn", [P, Q, B, C])
        tok2 = sb("tok2", [P, Q, B, C])
        xs = sb("xs", [P, Q, B, P], F32R)
        res = sb("res", [P, PAIRS, PIX])
        h1 = [sb(f"h1_{i}", [P, 512]) for i in range(3)]
        h2 = [sb(f"h2_{i}", [P, 512]) for i in range(3)]
        hch = xnorm[:].rearrange("p b n -> p (b n)").rearrange("p (k q n) -> p k q n", k=NK, q=Q)
        qch = act0[:].rearrange("p b n -> p (b n)").rearrange("p (k q n) -> p k q n", k=NK, q=Q)
        gated = norm0[:].rearrange("p b n -> p (b n)").rearrange("p (q c t) -> p q c t", q=Q, c=C)
        decay = xin[:].rearrange("p b n -> p (b n)").rearrange("p (q c t) -> p q c t", q=Q, c=C)
        yflat = y[:].rearrange("p b n -> p (b n)")
        ctxs = yflat[:, 0:2048].rearrange("p (q c t) -> p q c t", q=Q, c=C)
        xn2 = yflat[:, 2048:4096].rearrange("p (q b c) -> p q b c", q=Q, b=B)
        tok2ch = x1[:].rearrange("p b n -> p (b n)").rearrange("p (q b n) -> p q b n", q=Q, b=PAIRS)

        w1raw = sb("w1raw", [P, TAPS, P])
        w1hi = sb("w1hi", [P, TAPS, P], F32R)
        w1lo = sb("w1lo", [P, TAPS, P], F32R)
        f1hi = sb("f1hi", [P, EP, P], F32R)
        f1lo = sb("f1lo", [P, EP, P], F32R)
        f2s = sb("f2s", [P, EP, P])
        w3d = sb("w3d", [C, P])
        b3d = sb("b3d", [P, 1])
        expert_bias = sb("expert_bias", [E, C])
        wb = sb("wb", [P, Q, EP, P])
        minus_half = sb("minus_half", [P, 32])

        small_names = {}

        def tile(name, rows, *dims):
            n = 1
            for d in dims:
                n *= d
            if name not in small_names:
                small_names[name] = sb("s_" + name, [P, n])
            t = small_names[name][0:rows, 0:n]
            if len(dims) == 2:
                return t.rearrange("p (a b) -> p a b", a=dims[0])
            if len(dims) == 3:
                return t.rearrange("p (a b c) -> p a b c", a=dims[0], b=dims[1])
            return t

        bank = [ctx.enter_context(nc.psum_tensor(f"bank{i}", [P, 512], F32)) for i in range(8)]
        SMALL, XT = 4, 7

        def sem_list(*names):
            return [sem(n) for n in names]

        (x_loaded, params_loaded, conv1_w_loaded, out_stored) = sem_list(
            "x_loaded", "params_loaded", "conv1_w_loaded", "out_stored")
        vector_done = sem("vector_done")
        small_ready = sem("small_ready")
        small_free = sem("small_free")
        var_ready = sem("var_ready")
        rstd_ready = sem("rstd_ready")
        pads_zeroed = sem("pads_zeroed")
        consts_ready = sem("consts_ready")
        stats_ready = sem("stats_ready")
        xnorm_ready = sem("xnorm_ready")
        conv0_done = sem("conv0_done")
        act0_ready = sem("act0_ready")
        norm0_ready = sem("norm0_ready")
        pad_hi_ready = sem("pad_hi_ready")
        pad_lo_ready = sem("pad_lo_ready")
        w1_split = sem("w1_split")
        f1_split = sem("f1_split")
        conv1_done = sem("conv1_done")
        y_ready = sem("y_ready")
        gated_y_ready = sem("gated_y_ready")
        outconv_done = sem("outconv_done")
        x1_ready = sem("x1_ready")
        tok_in_psum = sem("tok_in_psum")
        tok_copied = sem("tok_copied")
        square_ready = sem("square_ready")
        hn_ready = sem("hn_ready")
        hch_in_psum = sem("hch_in_psum")
        hch_ready = sem("hch_ready")
        fc_done = sem("fc_done")
        qch_ready = sem("qch_ready")
        exps_in = sem("exps_in")
        exps_ready = sem("exps_ready")
        coef_ready = sem("coef_ready")
        decay_ready = sem("decay_ready")
        tok2_ready = sem("tok2_ready")
        square2_ready = sem("square2_ready")
        xn2_ready = sem("xn2_ready")
        xt_ready = sem("xt_ready")
        xs_hi = sem("xs_hi")
        xs_ready = sem("xs_ready")
        logits_ready = sem("logits_ready")
        wexp_ready = sem("wexp_ready")
        wt_ready = sem("wt_ready")
        t2_in_psum = sem("t2_in_psum")
        t2_copied = sem("t2_copied")
        z1_done = sem("z1_done")
        h1_ready = sem("h1_ready")
        z2_done = sem("z2_done")
        h2_ready = sem("h2_ready")
        mlp_done = sem("mlp_done")
        res_ready = sem("res_ready")

        order = ["s2row", "ebias", "gn1", ("gn2", 0), ("gn2", 1)]
        order += [(n, k) for k in range(NK) for n in ("gn3", "w2", "gna", "w3", "gn4", "score")]
        order += [(n, q) for q in range(Q) for n in ("logits", "wt", "wb", "ebt")]
        SMALL_AT = {name: i + 1 for i, name in enumerate(order)}
        order = ["bn", "gn1", ("gn2", 0), ("gn2", 1)]
        order += [(n, k) for k in range(NK) for n in ("gn3", "gna", "gn4", "ln1")]
        order += [("ln2", q) for q in range(Q)]
        VAR_AT = {name: i + 1 for i, name in enumerate(order)}
        order = ["bn", "gn1", ("gn2", 0), ("gn2", 1)]
        order += [(n, k) for k in range(NK) for n in ("gn3", "w2", "gna", "w3", "gn4")]
        STATS_AT = {name: i + 1 for i, name in enumerate(order)}

        var_tiles = {"bn": ("bnvar", P, 2 * EP), "gn1": ("gn1v", P, PAIRS)}
        for k in range(NK):
            var_tiles["gn2", k] = (f"gn2v{k}", P, PK)
            var_tiles["gn3", k] = (f"gn3v{k}", P, BK)
            var_tiles["gna", k] = (f"gnav{k}", C, BK)
            var_tiles["gn4", k] = (f"gn4v{k}", P, PK)
            var_tiles["ln1", k] = (f"ln1v{k}", P, Q * BK)
            var_tiles["ln2", k] = (f"ln2v{k}", P, B)

        def rstd(name):
            n, rows, cols = var_tiles[name]
            return tile(n + "r", rows, cols)

        def halves(k, q):
            return slice(k * PK, (k + 1) * PK), slice(q * P, (q + 1) * P)

        units = [(q, j, e, h) for q in range(Q) for j in range(NK) for e in range(EP) for h in range(2)]
        Z1, Z2, OUT = (2, 3), (5, 6), (0, 1)
        X1_UNIT, RES1_UNIT = 10, 14

        block = ctx.enter_context(nc.Block())

        @block.sync
        def _(sp):
            for b in range(PAIRS):
                sp.dma_start(xin[:, b, :], x_pairs[b]).then_inc(x_loaded, 16)
            for n in range(Q * NK):
                q, j = n // NK, n % NK
                pairs, pixels = halves(j, q)
                sp.wait_ge(res_ready, n + 1)
                sp.dma_start(out_pairs[pairs, :, pixels].rearrange("b p n -> p b n"),
                             res[:, pairs, pixels]).then_inc(out_stored, 16)
            sp.wait_ge(out_stored, 16 * Q * NK)

        @block.gpsimd
        def _(pool):
            nc.gpsimd.memset(minus_half[:], -0.5).then_inc(consts_ready, 1)
            for h in range(2):
                nc.gpsimd.memset(pad[h][:].bitcast(F32), 0.0).then_inc(pads_zeroed, 1)
            pool.wait_ge(consts_ready, 1)
            for name, at in VAR_AT.items():
                n, rows, cols = var_tiles[name]
                pool.wait_ge(var_ready, at)
                nc.gpsimd.tensor_tensor(rstd(name), tile(n, rows, cols), minus_half[0:rows, 0:cols],
                                        ALU.pow).then_inc(rstd_ready, 1)

        @block.scalar
        def _(act):
            act.dma_start(par[:], params).then_inc(params_loaded, 16)
            act.dma_start(w1raw[:], conv1_w).then_inc(conv1_w_loaded, 16)
            nc.scalar.preload_act_table(ACT.Silu)

            def silu0(k):
                for j in range(2):
                    act.wait_ge(conv0_done, 2 * k + j + 1)
                    b = k * PK + 2 * j
                    nc.scalar.activation(act0[:, b:b + 2, :], bank[(0, 1, 5, 6)[2 * k + j]][:].rearrange("p (b n) -> p b n", b=2),
                                         ACT.Silu, bias=w("b0")).then_inc(act0_ready, 1)

            def pad_high(k):
                act.wait_ge(norm0_ready, k + 1)
                act.wait_ge(pads_zeroed, 2)
                for h in range(2):
                    rows = slice(h * C, (h + 1) * C)
                    pairs = slice(k * PK, (k + 1) * PK)
                    nc.scalar.activation(pad[h][rows, pairs, 1:S + 1, 1:S + 1],
                                         norm0[rows, pairs, :].rearrange("p b (y x) -> p b y x", y=S),
                                         ACT.Copy).then_inc(pad_hi_ready, 1)

            def silu1(u):
                act.wait_ge(conv1_done, u + 1)
                k, j, h = u // 4, (u // 2) % 2, u % 2
                b = 2 * (k * PK + 2 * j) + h
                nc.scalar.activation(y[:, b:b + 3:2, :], bank[2 + u % 2][:].rearrange("p (b n) -> p b n", b=2),
                                     ACT.Silu, bias=w("b1")).then_inc(y_ready, 1)

            def window_silu(k):
                act.wait_ge(small_ready, SMALL_AT["w2", k])
                nc.scalar.activation(tile(f"wa{k}", C, 2, BK * WIN)[:, 0, :], bank[SMALL][0:C, 0:BK * WIN], ACT.Silu,
                                     bias=w("b2", C)).then_inc(small_free, 1)

            def window_tanh(k):
                act.wait_ge(small_ready, SMALL_AT["w3", k])
                nc.scalar.activation(tile(f"wt{k}", P, BK * WIN), bank[SMALL][:, 0:BK * WIN], ACT.Tanh,
                                     bias=b3d[:, 0:1], scale=0.5).then_inc(small_free, 1)

            def tok_copies(k):
                for q in range(Q):
                    act.wait_ge(tok_in_psum, Q * k + q + 1)
                    src = bank[q][:].rearrange("p (b c) -> p b c", c=C)
                    nc.scalar.activation(tok[:, q, k * BK:(k + 1) * BK, :], src, ACT.Copy).then_inc(tok_copied, 1)
                    nc.scalar.activation(square[:, q, k * BK:(k + 1) * BK, :], src, ACT.Square).then_inc(square_ready, 1)

            def hch_copies(k):
                for q in range(Q):
                    act.wait_ge(hch_in_psum, Q * k + q + 1)
                    nc.scalar.activation(hch[:, k, q, :], bank[5 + q][:], ACT.Copy).then_inc(hch_ready, 1)

            def fc_tanh(k):
                for q in range(Q):
                    act.wait_ge(fc_done, Q * k + q + 1)
                    nc.scalar.activation(qch[:, k, q, :], bank[(7, 0)[q]][:], ACT.Tanh, bias=w("fcb")).then_inc(qch_ready, 1)

            act.wait_ge(params_loaded, 16)
            silu0(0)
            silu0(1)
            pad_high(0)
            silu1(0)
            pad_high(1)
            for u in range(1, 4):
                silu1(u)
            window_silu(0)
            window_tanh(0)
            silu1(4)
            silu1(5)
            silu1(6)
            tok_copies(0)
            silu1(7)
            hch_copies(0)
            fc_tanh(0)
            window_silu(1)
            window_tanh(1)
            tok_copies(1)
            hch_copies(1)
            fc_tanh(1)
            act.wait_ge(exps_in, 1)
            nc.scalar.activation(tile("aexp", P, Q * 2 * B), tile("aarg", P, Q * 2 * B), ACT.Exp).then_inc(exps_ready, 1)
            for q in range(Q):
                if q == 0:
                    act.wait_ge(coef_ready, 1)
                nc.scalar.activation(decay[:, q], tile("coefa", P, Q, B)[:, q:q + 1, :].broadcast_to([P, C, B]),
                                     ACT.Copy).then_inc(decay_ready, 1)

            def squares2(q):
                act.wait_ge(tok2_ready, q + 1)
                nc.scalar.activation(square[:, q], tok2[:, q], ACT.Square).then_inc(square2_ready, 1)

            def high_x(q):
                for g in range(NK):
                    act.wait_ge(xt_ready, NK * q + g + 1)
                    for h in range(2):
                        own = slice(h * C, (h + 1) * C)
                        nc.scalar.activation(xs[own, q, g * BK + h:(g + 1) * BK:2, :],
                                             bank[XT][own, :].rearrange("p (b n) -> p b n", b=PK), ACT.Copy).then_inc(xs_hi, 1)

            def route(q):
                act.wait_ge(logits_ready, q + 1)
                nc.scalar.activation(tile(f"wexp{q}", P, E), tile(f"lg{q}", P, E), ACT.Exp,
                                     bias=tile(f"lmax{q}", P, 1), accum_out=tile(f"lsum{q}", P, 1)).then_inc(wexp_ready, 1)
                act.wait_ge(small_ready, SMALL_AT["wb", q])
                nc.scalar.activation(wb[:, q], bank[SMALL][:].rearrange("p (e n) -> p e n", e=EP),
                                     ACT.Copy).then_inc(small_free, 1)

            def residual_copies(q):
                for j in range(NK):
                    act.wait_ge(t2_in_psum, NK * q + j + 1)
                    nc.scalar.activation(tok2ch[:, q, j * PK:(j + 1) * PK, :], bank[XT][:].rearrange("p (b n) -> p b n", b=PK),
                                         ACT.Copy).then_inc(t2_copied, 1)

            def relu1(n):
                act.wait_ge(z1_done, n + 1)
                if n >= 3:
                    act.wait_ge(z2_done, n - 2)
                e = units[n][2]
                nc.scalar.activation(h1[n % 3][:], bank[Z1[n % 2]][:], ACT.Relu, bias=tile("bnb", P, 2 * EP)[:, e:e + 1],
                                     scale=tile("bns", P, 2 * EP)[:, e:e + 1]).then_inc(h1_ready, 1)

            squares2(0)
            high_x(0)
            route(0)
            squares2(1)
            for n in range(len(units)):
                relu1(n)
                if n == 1:
                    residual_copies(0)
                if n == X1_UNIT - 1:
                    high_x(1)
                if n == X1_UNIT + 1:
                    route(1)
                if n == RES1_UNIT - 1:
                    residual_copies(1)

        @block.vector
        def _(dve):
            steps = [0]

            def step(ins):
                steps[0] += 1
                ins.then_inc(vector_done, 1)
                dve.wait_ge(vector_done, steps[0])

            V = nc.vector

            def group_finish(name, n, rows=P):
                t, _, _ = var_tiles[name]
                ms, sq = tile(t + "ms", rows, 2, n), tile(t + "sq", rows, n)
                dve.wait_ge(small_ready, SMALL_AT[name])
                V.tensor_copy(ms, bank[SMALL][0:rows, 0:2 * n].rearrange("p (a n) -> p a n", a=2)).then_inc(small_free, 1)
                dve.wait_ge(small_free, SMALL_AT[name])
                step(V.tensor_tensor(sq, ms[:, 0, :], ms[:, 0, :], ALU.mult))
                V.scalar_tensor_tensor(tile(t, rows, n), ms[:, 1, :], EPS, sq, ALU.add, ALU.subtract).then_inc(var_ready, 1)

            def group_shift(name, n, rows=P):
                t, _, _ = var_tiles[name]
                dve.wait_ge(rstd_ready, VAR_AT[name])
                step(V.scalar_tensor_tensor(tile(t + "nb", rows, n), tile(t + "ms", rows, 2, n)[:, 0, :], -1.0, rstd(name),
                                            ALU.mult, ALU.mult))
                return rstd(name), tile(t + "nb", rows, n)

            def channel_stats(name, source, n):
                t, _, _ = var_tiles[name]
                raw, mv, e2 = tile(t + "raw", P, n, 6), tile(t + "mv", P, n, 2), tile(t + "e2", P, 2, n)
                for i in range(n):
                    ins = V.bn_stats(raw[:, i, :], source(i))
                step(ins)
                for i in range(n):
                    ins = V.bn_aggr(mv[:, i, :], raw[:, i, :])
                step(ins)
                V.tensor_copy(e2[:, 0, :], mv[:, :, 0])
                step(V.tensor_tensor(e2[:, 1, :], mv[:, :, 0], mv[:, :, 0], ALU.mult))
                V.tensor_tensor(e2[:, 1, :], e2[:, 1, :], mv[:, :, 1], ALU.add).then_inc(stats_ready, 1)

            t = "gn1v"
            raw, mv, e2 = tile(t + "raw", P, PAIRS, 6), tile(t + "mv", P, PAIRS, 2), tile(t + "e2", P, 2, PAIRS)
            dve.wait_ge(params_loaded, 16)
            bn1, bn2 = (w(n).rearrange("p (a e) -> p a e", a=5) for n in ("bn1", "bn2"))
            bnvar = tile("bnvar", P, 2 * EP)
            V.tensor_scalar(bnvar[:, 0:EP], bn1[:, 4, :], BN_EPS, None, ALU.add)
            V.tensor_scalar(bnvar[:, EP:2 * EP], bn2[:, 4, :], BN_EPS, None, ALU.add).then_inc(var_ready, 1)
            dve.wait_ge(x_loaded, 16 * PAIRS)
            for b in range(PAIRS):
                ins = V.bn_stats(raw[:, b, :], xin[:, b, :])
            step(ins)
            for b in range(PAIRS):
                ins = V.bn_aggr(mv[:, b, :], raw[:, b, :])
            step(ins)
            V.tensor_copy(e2[:, 0, :], mv[:, :, 0])
            step(V.tensor_tensor(e2[:, 1, :], mv[:, :, 0], mv[:, :, 0], ALU.mult))
            bns, bnb = tile("bns", P, 2 * EP), tile("bnb", P, 2 * EP)
            dve.wait_ge(rstd_ready, VAR_AT["bn"])
            r = rstd("bn")
            V.tensor_tensor(bns[:, 0:EP], bn1[:, 1, :], r[:, 0:EP], ALU.mult)
            V.tensor_tensor(bns[:, EP:2 * EP], bn2[:, 1, :], r[:, EP:2 * EP], ALU.mult)
            V.tensor_tensor(bnb[:, 0:EP], bn1[:, 0, :], bn1[:, 3, :], ALU.subtract)
            step(V.tensor_tensor(bnb[:, EP:2 * EP], bn2[:, 0, :], bn2[:, 3, :], ALU.subtract))
            step(V.tensor_tensor(bnb, bnb, bns, ALU.mult))
            V.tensor_tensor(bnb[:, 0:EP], bnb[:, 0:EP], bn1[:, 2, :], ALU.add)
            step(V.tensor_tensor(bnb[:, EP:2 * EP], bnb[:, EP:2 * EP], bn2[:, 2, :], ALU.add))
            diag = tile("diag", P, EP, P)
            for e in range(EP):
                V.tensor_scalar(diag[:, e, :], w("ident"), bns[:, EP + e:EP + e + 1], None, ALU.mult)
            V.tensor_tensor(tile("bcol", P, EP, E), w("emask").rearrange("p (e m) -> p e m", e=EP),
                            bnb[:, EP:2 * EP].rearrange("p (e o) -> p e o", o=1).broadcast_to([P, EP, E]), ALU.mult)
            step(V.tensor_scalar(tile("negb", P, EP), bnb[:, EP:2 * EP], -1.0, None, ALU.mult))
            V.tensor_tensor(w3d[:], w("w3", C)[:, 0:P], w("w3", C)[:, P:2 * P], ALU.subtract)
            step(V.tensor_tensor(b3d[:], w("b3")[:, 0:1], w("b3")[:, 1:2], ALU.subtract))
            V.tensor_scalar(b3d[:], b3d[:], 0.5, None, ALU.mult).then_inc(stats_ready, 1)
            V.tensor_tensor(e2[:, 1, :], e2[:, 1, :], mv[:, :, 1], ALU.add).then_inc(stats_ready, 1)
            dve.wait_ge(small_ready, SMALL_AT["s2row"])
            V.tensor_tensor(f2s[:], w("ffn2").rearrange("p (e m) -> p e m", e=EP),
                            bank[SMALL][:].rearrange("p (e m) -> p e m", e=EP), ALU.mult).then_inc(small_free, 1)
            dve.wait_ge(small_ready, SMALL_AT["ebias"])
            V.tensor_copy(expert_bias[:], bank[SMALL][0:E, 0:C]).then_inc(small_free, 1)
            dve.wait_ge(small_free, 2)
            group_finish("gn1", PAIRS)
            r, nb = group_shift("gn1", PAIRS)
            for b in range(PAIRS):
                V.tensor_scalar(xnorm[:, b, :], xin[:, b, :], r[:, b:b + 1], nb[:, b:b + 1],
                                ALU.mult, ALU.add).then_inc(xnorm_ready, 1)

            dve.wait_ge(conv1_w_loaded, 16)
            step(V.tensor_copy(w1hi[:], w1raw[:]))
            V.tensor_tensor(w1lo[:], w1raw[:], w1hi[:].bitcast(F32), ALU.subtract).then_inc(w1_split, 1)

            def norm_stage0(k):
                dve.wait_ge(act0_ready, 2 * k + 2)
                channel_stats(("gn2", k), lambda i: act0[:, k * PK + i, :], PK)
                group_finish(("gn2", k), PK)
                r, nb = group_shift(("gn2", k), PK)
                for i in range(PK):
                    ins = V.tensor_scalar(norm0[:, k * PK + i, :], act0[:, k * PK + i, :], r[:, i:i + 1], nb[:, i:i + 1],
                                          ALU.mult, ALU.add)
                ins.then_inc(norm0_ready, 1)
                dve.wait_ge(norm0_ready, k + 1)
                for h in range(2):
                    dve.wait_ge(pad_hi_ready, 2 * k + h + 1)
                    own, other = slice(h * C, (h + 1) * C), slice((1 - h) * C, (2 - h) * C)
                    for j in range(2):
                        pairs = slice(k * PK + 2 * j, k * PK + 2 * j + 2)
                        V.tensor_tensor(pad[h][other, pairs, 1:S + 1, 1:S + 1],
                                        norm0[own, pairs, :].rearrange("p b (y x) -> p b y x", y=S),
                                        pad[h][own, pairs, 1:S + 1, 1:S + 1].bitcast(F32), ALU.subtract).then_inc(pad_lo_ready, 1)

            def window_stats(u):
                dve.wait_ge(y_ready, u + 1)
                k, j, h = u // 4, (u // 2) % 2, u % 2
                ws = tile(f"ws{k}", P, BK * WIN, 6)
                for i in range(2):
                    b = 2 * (2 * j + i) + h
                    img = y[:, k * BK + b, :].rearrange("p (a y c x) -> p a y c x", a=2, y=8, c=2)
                    for n in range(WIN):
                        ins = V.bn_stats(ws[:, b * WIN + n, :], img[:, n // 2, :, n % 2, :])
                step(ins)

            def gn3_stats(k):
                n = BK * WIN
                ws = tile(f"ws{k}", P, n, 6)
                st, sq, sm = tile(f"wst{k}", P, 2, n), tile(f"wsq{k}", P, n, 2), tile(f"wsm{k}", P, 2, n)
                means = ws.rearrange("p n (a t) -> p n a t", a=2)[:, :, :, 1]
                V.tensor_tensor(sq, means, means, ALU.mult)
                V.tensor_tensor(st[:, 0, :], ws[:, :, 1], ws[:, :, 4], ALU.add)
                step(V.tensor_tensor(sm[:, 0, :], ws[:, :, 2], ws[:, :, 5], ALU.add))
                step(V.tensor_tensor(sm[:, 1, :], sq[:, :, 0], sq[:, :, 1], ALU.add))
                step(V.scalar_tensor_tensor(st[:, 1, :], sm[:, 0, :], 1.0 / 32, sm[:, 1, :], ALU.mult, ALU.add))
                V.tensor_reduce(tile(f"wsum{k}", P, 2 * BK), st.rearrange("p a (b n) -> p (a b) n", n=WIN), AX_X,
                                ALU.add).then_inc(stats_ready, 1)

            def window_in(k):
                r, nb = group_shift(("gn3", k), BK)
                st = tile(f"wst{k}", P, 2, BK * WIN)
                a = tile(f"win{k}", P, BK, WIN)
                each = lambda t, rows=P: t.rearrange("p (b o) -> p b o", o=1).broadcast_to([rows, BK, WIN])
                step(V.scalar_tensor_tensor(a, st[:, 0, :].rearrange("p (b n) -> p b n", n=WIN), 0.5, each(r), ALU.mult, ALU.mult))
                step(V.tensor_tensor(a, a, each(nb), ALU.add))
                other = tile(f"wino{k}", C, BK, WIN)
                step(V.tensor_copy(other, a[C:P]))
                V.tensor_tensor(tile(f"wmax{k}", C, BK, WIN), a[0:C], other, ALU.max).then_inc(stats_ready, 1)

            def normalise_y(k):
                r, nb = rstd(("gn3", k)), tile(f"gn3v{k}nb", P, BK)
                for b in range(BK):
                    ins = V.tensor_scalar(y[:, k * BK + b, :], y[:, k * BK + b, :], r[:, b:b + 1], nb[:, b:b + 1],
                                          ALU.mult, ALU.add)
                step(ins)

            def window_norm_stats(k):
                wa = tile(f"wa{k}", C, 2, BK * WIN)
                dve.wait_ge(small_free, SMALL_AT["w2", k])
                step(V.tensor_tensor(wa[:, 1, :], wa[:, 0, :], wa[:, 0, :], ALU.mult))
                V.tensor_reduce(tile(f"wr{k}", C, 2 * BK), wa.rearrange("p a (b n) -> p (a b) n", n=WIN), AX_X,
                                ALU.add).then_inc(stats_ready, 1)

            def window_normalise(k):
                group_finish(("gna", k), BK, C)
                r, nb = group_shift(("gna", k), BK, C)
                a = tile(f"wa{k}", C, 2, BK * WIN)[:, 0, :].rearrange("p (b n) -> p b n", n=WIN)
                each = lambda t: t.rearrange("p (b o) -> p b o", o=1).broadcast_to([C, BK, WIN])
                an = tile(f"wan{k}", C, BK, WIN)
                step(V.tensor_tensor(an, a, each(r), ALU.mult))
                V.tensor_tensor(an, an, each(nb), ALU.add).then_inc(stats_ready, 1)

            def gate_y(k):
                dve.wait_ge(small_free, SMALL_AT["w3", k])
                g = tile(f"gate{k}", P, BK * 2, S)
                step(V.tensor_scalar(g.rearrange("p n (c x) -> p (n c) x", c=2),
                                     tile(f"wt{k}", P, BK * WIN).rearrange("p (n o) -> p n o", o=1).broadcast_to([P, BK * WIN, 8]),
                                     0.5, 0.5, ALU.mult, ALU.add))
                for j in range(2):
                    yk = y[:, k * BK + 4 * j:k * BK + 4 * j + 4, :].rearrange("p b (a y x) -> p (b a) y x", a=2, y=8)
                    gj = g[:, 8 * j:8 * j + 8, :]
                    V.tensor_tensor(yk, yk, gj.rearrange("p n (o x) -> p n o x", o=1).broadcast_to([P, BK, 8, S]),
                                    ALU.mult).then_inc(gated_y_ready, 1)

            def residual1(k):
                dve.wait_ge(outconv_done, 2 * k + 2)
                image = lambda i: bank[5 + i // 2][:, (i % 2) * PIX:(i % 2 + 1) * PIX]
                channel_stats(("gn4", k), image, PK)
                group_finish(("gn4", k), PK)
                r, nb = group_shift(("gn4", k), PK)
                for i in range(PK):
                    ins = V.tensor_scalar(xin[:, k * PK + i, :], xin[:, k * PK + i, :], nb[:, i:i + 1], None, ALU.add)
                step(ins)
                for i in range(PK):
                    ins = V.scalar_tensor_tensor(x1[:, k * PK + i, :], image(i), r[:, i:i + 1], xin[:, k * PK + i, :],
                                                 ALU.mult, ALU.add)
                ins.then_inc(x1_ready, 1)

            def layer_norm_stats(name, source, squares, n):
                t, _, _ = var_tiles[name]
                s, m, v = tile(t + "s", P, 2, n), tile(t + "m", P, n), tile(t, P, n)
                V.tensor_reduce(s[:, 0, :], source, AX_X, ALU.add)
                step(V.tensor_reduce(s[:, 1, :], squares, AX_X, ALU.add))
                step(V.tensor_scalar(s, s, 1.0 / C, None, ALU.mult))
                step(V.tensor_tensor(m, s[:, 0, :], s[:, 0, :], ALU.mult))
                V.scalar_tensor_tensor(v, s[:, 1, :], EPS, m, ALU.add, ALU.subtract).then_inc(var_ready, 1)

            def layer_norm_1(k):
                dve.wait_ge(tok_copied, Q * (k + 1))
                dve.wait_ge(square_ready, Q * (k + 1))
                samples = slice(k * BK, (k + 1) * BK)
                n = Q * BK
                t = f"ln1v{k}"
                s, m, v = tile(t + "s", P, 2, n), tile(t + "m", P, n), tile(t, P, n)
                for q in range(Q):
                    V.tensor_reduce(s[:, 0, q * BK:(q + 1) * BK], tok[:, q, samples, :], AX_X, ALU.add)
                    ins = V.tensor_reduce(s[:, 1, q * BK:(q + 1) * BK], square[:, q, samples, :], AX_X, ALU.add)
                step(ins)
                step(V.tensor_scalar(s, s, 1.0 / C, None, ALU.mult))
                step(V.tensor_tensor(m, s[:, 0, :], s[:, 0, :], ALU.mult))
                V.scalar_tensor_tensor(v, s[:, 1, :], EPS, m, ALU.add, ALU.subtract).then_inc(var_ready, 1)
                each = lambda a: a.rearrange("p (b o) -> p b o", o=1).broadcast_to([P, BK, C])
                for q in range(Q):
                    ins = V.tensor_tensor(hn[:, q, samples, :], tok[:, q, samples, :], each(s[:, 0, q * BK:(q + 1) * BK]), ALU.subtract)
                step(ins)
                dve.wait_ge(rstd_ready, VAR_AT["ln1", k])
                r = rstd(("ln1", k))
                for q in range(Q):
                    V.tensor_tensor(hn[:, q, samples, :], hn[:, q, samples, :], each(r[:, q * BK:(q + 1) * BK]),
                                    ALU.mult).then_inc(hn_ready, 1)

            scores = tile("scores", P, Q, B)

            def take_scores(k):
                dve.wait_ge(small_ready, SMALL_AT["score", k])
                V.tensor_copy(scores[:, :, k * BK:(k + 1) * BK],
                              bank[SMALL][:, 0:Q * BK].rearrange("p (q b) -> p q b", q=Q)).then_inc(small_free, 1)
                dve.wait_ge(small_free, SMALL_AT["score", k])

            def attention_coefficients():
                m = tile("runmax", P, Q, B + 1)
                step(V.memset(m[:, :, 0:1], LOWEST))
                for q in range(Q):
                    ins = V.tensor_tensor_scan(m[:, q, 1:B + 1], scores[:, q, :], scores[:, q, :], LOWEST, ALU.max, ALU.max)
                step(ins)
                arg = tile("aarg", P, 2, Q * B)
                V.tensor_tensor(arg[:, 0, :].rearrange("p (q b) -> p q b", q=Q), m[:, :, 0:B], m[:, :, 1:B + 1], ALU.subtract)
                V.tensor_tensor(arg[:, 1, :].rearrange("p (q b) -> p q b", q=Q), scores, m[:, :, 1:B + 1],
                                ALU.subtract).then_inc(exps_in, 1)
                dve.wait_ge(exps_ready, 1)
                ex = tile("aexp", P, 2, Q * B)
                runsum = tile("runsum", P, Q * B + 1)
                inv, b_, a_ = tile("inv", P, Q * B), tile("coefb", P, Q * B), tile("coefa", P, Q * B)
                V.memset(runsum[:, 0:1], 0.0)
                step(V.tensor_tensor_scan(runsum[:, 1:], ex[:, 0, :], ex[:, 1, :], 0.0, ALU.mult, ALU.add))
                V.tensor_tensor(a_, ex[:, 0, :], runsum[:, 0:Q * B], ALU.mult)
                step(V.reciprocal(inv, runsum[:, 1:]))
                V.tensor_tensor(b_, ex[:, 1, :], inv, ALU.mult)
                V.tensor_tensor(a_, a_, inv, ALU.mult).then_inc(coef_ready, 1)
                dve.wait_ge(coef_ready, 1)

            def attend(q):
                b_ = tile("coefb", P, Q, B)
                step(V.tensor_tensor(gated[:, q], hn[:, q].rearrange("p b c -> p c b"),
                                     b_[:, q:q + 1, :].broadcast_to([P, C, B]), ALU.mult))
                dve.wait_ge(decay_ready, q + 1)
                flat = lambda t: t[:, q].rearrange("p c b -> p (c b)")
                step(V.tensor_tensor_scan(flat(ctxs), flat(decay), flat(gated), 0.0, ALU.mult, ALU.add))
                V.tensor_tensor(tok2[:, q], tok[:, q], ctxs[:, q].rearrange("p c b -> p b c"), ALU.add).then_inc(tok2_ready, 1)
                dve.wait_ge(tok2_ready, q + 1)

            def layer_norm_2(q):
                dve.wait_ge(square2_ready, q + 1)
                t = f"ln2v{q}"
                layer_norm_stats(("ln2", q), tok2[:, q], square[:, q], B)
                each = lambda a: a.rearrange("p (b o) -> p b o", o=1).broadcast_to([P, B, C])
                step(V.tensor_tensor(xn2[:, q], tok2[:, q], each(tile(t + "s", P, 2, B)[:, 0, :]), ALU.subtract))
                dve.wait_ge(rstd_ready, VAR_AT["ln2", q])
                V.tensor_tensor(xn2[:, q], xn2[:, q], each(rstd(("ln2", q))), ALU.mult).then_inc(xn2_ready, 1)

            def split_x(q, g):
                dve.wait_ge(xs_hi, 4 * q + 2 * g + 2)
                for h in range(2):
                    own, other = slice(h * C, (h + 1) * C), slice((1 - h) * C, (2 - h) * C)
                    samples = slice(g * BK + h, (g + 1) * BK, 2)
                    V.tensor_tensor(xs[other, q, samples, :], bank[XT][own, :].rearrange("p (b n) -> p b n", b=PK),
                                    xs[own, q, samples, :].bitcast(F32), ALU.subtract).then_inc(xs_ready, 1)

            def route(q):
                lg, mx = tile(f"lg{q}", P, E), tile(f"lmax{q}", P, 1)
                dve.wait_ge(small_ready, SMALL_AT["logits", q])
                V.scalar_tensor_tensor(lg, bank[SMALL][:, 0:E], 1.0 / B, w("br"), ALU.mult, ALU.add).then_inc(small_free, 1)
                dve.wait_ge(small_free, SMALL_AT["logits", q])
                V.tensor_reduce(mx, lg, AX_X, ALU.max, negate=True).then_inc(logits_ready, 1)
                dve.wait_ge(wexp_ready, q + 1)
                step(V.reciprocal(tile(f"linv{q}", P, 1), tile(f"lsum{q}", P, 1)))
                V.tensor_scalar(tile(f"wsoft{q}", P, E), tile(f"wexp{q}", P, E), tile(f"linv{q}", P, 1), None,
                                ALU.mult).then_inc(wt_ready, 1)
                dve.wait_ge(small_ready, SMALL_AT["wt", q])
                V.tensor_copy(tile(f"wT{q}", E, P), bank[SMALL][0:E, 0:P]).then_inc(small_free, 1)

            def add_expert_bias(q):
                dve.wait_ge(small_ready, SMALL_AT["ebt", q])
                V.tensor_tensor(tok2[:, q], tok2[:, q],
                                bank[SMALL][:, 0:C].rearrange("p (o c) -> p o c", o=1).broadcast_to([P, B, C]),
                                ALU.add).then_inc(small_free, 1)

            def weigh(n):
                q, j, e, h = units[n]
                dve.wait_ge(z2_done, n + 1)
                if n == 0 or units[n - 1][0] != q:
                    dve.wait_ge(small_free, SMALL_AT["wb", q])
                if n >= 3:
                    dve.wait_ge(mlp_done, n - 2)
                V.scalar_tensor_tensor(h2[n % 3][:].rearrange("p (b n) -> p b n", b=PK),
                                       bank[Z2[n % 2]][:].rearrange("p (b n) -> p b n", b=PK), tile("negb", P, EP)[:, e:e + 1],
                                       wb[:, q, e:e + 1, :].broadcast_to([P, PK, P]), ALU.max, ALU.mult).then_inc(h2_ready, 1)

            def finish(m):
                q, j = m // NK, m % NK
                dve.wait_ge(mlp_done, 8 * (m + 1))
                dve.wait_ge(t2_copied, m + 1)
                pairs, pixels = halves(j, q)
                V.tensor_tensor(res[:, pairs, pixels], bank[OUT[m % 2]][:].rearrange("p (b n) -> p b n", b=PK),
                                tok2ch[:, q, pairs, :], ALU.add).then_inc(res_ready, 1)

            norm_stage0(0)
            norm_stage0(1)
            f1 = w("ffn1").rearrange("p (e m) -> p e m", e=EP)
            step(V.tensor_copy(f1hi[:], f1))
            V.tensor_tensor(f1lo[:], f1, f1hi[:].bitcast(F32), ALU.subtract).then_inc(f1_split, 1)
            for u in range(4):
                window_stats(u)
            gn3_stats(0)
            group_finish(("gn3", 0), BK)
            window_in(0)
            normalise_y(0)
            window_norm_stats(0)
            window_normalise(0)
            gate_y(0)
            window_stats(4)
            window_stats(5)
            residual1(0)
            window_stats(6)
            layer_norm_1(0)
            window_stats(7)
            gn3_stats(1)
            take_scores(0)
            group_finish(("gn3", 1), BK)
            window_in(1)
            normalise_y(1)
            window_norm_stats(1)
            window_normalise(1)
            gate_y(1)
            residual1(1)
            layer_norm_1(1)
            take_scores(1)
            attention_coefficients()
            attend(0)
            layer_norm_2(0)
            for g in range(NK):
                split_x(0, g)
            route(0)
            add_expert_bias(0)
            attend(1)
            for n in range(len(units)):
                weigh(n)
                if n == 0:
                    layer_norm_2(1)
                if n % 8 == 7:
                    finish(n // 8)
                if n == X1_UNIT - 3:
                    for g in range(NK):
                        split_x(1, g)
                if n == X1_UNIT - 1:
                    route(1)
                    add_expert_bias(1)

        @block.tensor
        def _(pe):
            T = nc.tensor

            def small(name, *also):
                if SMALL_AT[name] > 1:
                    pe.wait_ge(small_free, SMALL_AT[name] - 1)

            def group_product(name, matrix, rhs, rows, n):
                small(name)
                pe.wait_ge(stats_ready, STATS_AT[name])
                T.matmul(bank[SMALL][0:rows, 0:n], matrix, rhs, start=True, stop=True).then_inc(small_ready, 1)

            pe.wait_ge(params_loaded, 16)
            pe.wait_ge(stats_ready, STATS_AT["bn"])
            T.matmul(bank[SMALL][:], w("ones"), tile("diag", P, EP * P), start=True, stop=True).then_inc(small_ready, 1)
            small("ebias")
            wo = w("ffo").rearrange("p (e m) -> p e m", e=EP)
            for e in range(EP):
                T.matmul(bank[SMALL][0:E, 0:C], tile("bcol", P, EP, E)[:, e, :], wo[:, e, :], start=(e == 0), stop=False)
            T.matmul(bank[SMALL][0:E, 0:C], w("ident", E)[:, 0:E], w("bo", E), start=False, stop=True).then_inc(small_ready, 1)
            group_product("gn1", w("gn1"), tile("gn1ve2", P, 2 * PAIRS), P, 2 * PAIRS)
            for j in range(PAIRS // 2):
                pe.wait_ge(xnorm_ready, 2 * j + 2)
                T.matmul(bank[(0, 1, 5, 6)[j]][:], w("w0"), xnorm[:, 2 * j:2 * j + 2, :], start=True, stop=True).then_inc(conv0_done, 1)
            for k in range(NK):
                if k == 0:
                    group_product(("gn2", k), w("gn2"), tile(f"gn2v{k}e2", P, 2 * PK), P, 2 * PK)
                    pe.wait_ge(w1_split, 1)

            def conv1(u, part):
                k, j, h = u // 4, (u // 2) % 2, u % 2
                if part == 0:
                    pe.wait_ge(pad_lo_ready, 4 * k + 2 * h + j + 1)
                    if u >= 2:
                        pe.wait_ge(y_ready, u - 1)
                b = k * PK + 2 * j
                taps = range(0, 5) if part == 0 else range(5, TAPS)
                for tap in taps:
                    dy, dx = tap // 3, tap % 3
                    for weights in (w1hi, w1lo):
                        ins = T.matmul(bank[2 + u % 2][:], weights[:, tap, :], pad[h][:, b:b + 2, dy:dy + S, dx:dx + S],
                                       start=(tap == 0 and weights is w1hi), stop=(tap == TAPS - 1 and weights is w1lo))
                if part == 1:
                    ins.then_inc(conv1_done, 1)

            def out_product(k):
                for j in range(2):
                    pe.wait_ge(gated_y_ready, 2 * k + j + 1)
                    if k:
                        pe.wait_ge(hch_ready, 2 * k)
                    b = k * BK + 4 * j
                    for h in range(2):
                        ins = T.matmul(bank[5 + j][h * C:(h + 1) * C, :], w("weight"), y[:, b + h:b + h + 3:2, :], start=True, stop=True)
                    ins.then_inc(outconv_done, 1)

            def to_tokens(k):
                pe.wait_ge(x1_ready, k + 1)
                if k:
                    pe.wait_ge(qch_ready, 2)
                for q in range(Q):
                    for i in range(PK):
                        ins = T.transpose(bank[q][:, i * P:(i + 1) * P], x1[:, k * PK + i, q * P:(q + 1) * P], w("ident"))
                    ins.then_inc(tok_in_psum, 1)

            def to_channels(k):
                for q in range(Q):
                    pe.wait_ge(hn_ready, Q * k + q + 1)
                    for i in range(PK):
                        b = k * BK + 2 * i
                        ins = T.transpose(bank[5 + q][:, i * P:(i + 1) * P], hn[:, q, b:b + 2, :].rearrange("p b c -> p (b c)"), w("ident"))
                    ins.then_inc(hch_in_psum, 1)

            def fc(k):
                for q in range(Q):
                    pe.wait_ge(hch_ready, Q * k + q + 1)
                    if q == 1:
                        pe.wait_ge(tok_copied, Q * (k + 1))
                        pe.wait_ge(square_ready, Q * (k + 1))
                    elif k:
                        pe.wait_ge(qch_ready, Q * (k - 1) + q + 1)
                    T.matmul(bank[(7, 0)[q]][:], w("fc"), hch[:, k, q, :], start=True, stop=True).then_inc(fc_done, 1)

            def score(k):
                small(("score", k))
                for q in range(Q):
                    pe.wait_ge(qch_ready, Q * k + q + 1)
                    for i in range(PK):
                        at = q * BK + 2 * i
                        ins = T.matmul(bank[SMALL][:, at:at + 2], qch[:, k, q, i * P:(i + 1) * P], w("score"), start=True, stop=True)
                ins.then_inc(small_ready, 1)

            def window_steps(k):
                return [
                    lambda: group_product(("gn3", k), w("gn3"), tile(f"wsum{k}", P, 2 * BK), P, 2 * BK),
                    lambda: group_product(("w2", k), w("w2", C), tile(f"wmax{k}", C, BK * WIN), C, BK * WIN),
                    lambda: group_product(("gna", k), w("gna", C), tile(f"wr{k}", C, 2 * BK), C, 2 * BK),
                    lambda: group_product(("w3", k), w3d[:], tile(f"wan{k}", C, BK * WIN), P, BK * WIN),
                    lambda: out_product(k),
                    lambda: group_product(("gn4", k), w("gn1"), tile(f"gn4v{k}e2", P, 2 * PK), P, 2 * PK),
                    lambda: to_tokens(k),
                    lambda: to_channels(k),
                    lambda: (fc(k), score(k)),
                ]

            conv1(0, 0)
            conv1(0, 1)
            group_product(("gn2", 1), w("gn2"), tile("gn2v1e2", P, 2 * PK), P, 2 * PK)
            for u in range(1, 4):
                conv1(u, 0)
                conv1(u, 1)
            chain = window_steps(0)
            for u in range(4, 8):
                for part in range(2):
                    conv1(u, part)
                    chain.pop(0)()
            for go in chain + window_steps(1):
                go()

            def x_transposes(q, g):
                if g == 0:
                    pe.wait_ge(xn2_ready, q + 1)
                    if q == 0:
                        pe.wait_ge(qch_ready, 4)
                    else:
                        pe.wait_ge(t2_copied, 2)
                else:
                    pe.wait_ge(xs_ready, 4 * q + 2 * g)
                for i in range(PK):
                    b = g * BK + 2 * i
                    src = xn2[:, q, b:b + 2, :].rearrange("p b c -> p (b c)")
                    ins = T.transpose(bank[XT][:, i * P:(i + 1) * P], src, w("ident"))
                ins.then_inc(xt_ready, 1)

            def logits(q):
                small(("logits", q))
                pe.wait_ge(xs_ready, 4 * q + 4)
                for b in range(B):
                    ins = T.matmul(bank[SMALL][:, 0:E], xs[:, q, b, :].bitcast(F32), w("wr"), start=(b == 0), stop=(b == B - 1))
                ins.then_inc(small_ready, 1)

            def weights_transposed(q):
                small(("wt", q))
                pe.wait_ge(wt_ready, q + 1)
                T.transpose(bank[SMALL][0:E, 0:P], tile(f"wsoft{q}", P, E), w("ident")).then_inc(small_ready, 1)

            def weights_spread(q):
                small(("wb", q))
                wt = tile(f"wT{q}", E, P)
                for e in range(EP):
                    ins = T.matmul(bank[SMALL][:, e * P:(e + 1) * P], w("sel", E)[:, e * P:(e + 1) * P], wt, start=True, stop=True)
                ins.then_inc(small_ready, 1)

            def expert_bias_tokens(q):
                small(("ebt", q))
                T.matmul(bank[SMALL][:, 0:C], tile(f"wT{q}", E, P), expert_bias[:], start=True, stop=True).then_inc(small_ready, 1)

            def residual_transposes(q, j):
                if j == 0:
                    pe.wait_ge(small_free, SMALL_AT["ebt", q])
                    pe.wait_ge(xs_ready, 4 * q + 4)
                else:
                    pe.wait_ge(t2_copied, NK * q + j)
                for i in range(PK):
                    b = 2 * (j * PK + i)
                    ins = T.transpose(bank[XT][:, i * P:(i + 1) * P], tok2[:, q, b:b + 2, :].rearrange("p b c -> p (b c)"), w("ident"))
                ins.then_inc(t2_in_psum, 1)

            def layer1(n):
                q, j, e, h = units[n]
                if n >= 2:
                    pe.wait_ge(h1_ready, n - 1)
                xq = xs[:, q, 2 * j * PK + h:2 * (j + 1) * PK:2, :]
                for m, weights in enumerate((f1hi, f1lo)):
                    ins = T.matmul(bank[Z1[n % 2]][:], weights[:, e, :], xq, start=(m == 0), stop=(m == 1))
                ins.then_inc(z1_done, 1)

            def layer2(n):
                e = units[n][2]
                pe.wait_ge(h1_ready, n + 1)
                if n >= 2:
                    pe.wait_ge(h2_ready, n - 1)
                T.matmul(bank[Z2[n % 2]][:], f2s[:, e, :], h1[n % 3][:], start=True, stop=True).then_inc(z2_done, 1)

            def layer3(n):
                q, j, e, h = units[n]
                m = n // 8
                pe.wait_ge(h2_ready, n + 1)
                if n % 8 == 0 and m >= 2:
                    pe.wait_ge(res_ready, m - 1)
                T.matmul(bank[OUT[m % 2]][h * C:(h + 1) * C, :], wo[:, e, :], h2[n % 3][:], start=(e == 0), stop=(e == EP - 1),
                         ).then_inc(mlp_done, 1)

            for g in range(NK):
                x_transposes(0, g)
            pe.wait_ge(f1_split, 1)
            logits(0)
            weights_transposed(0)
            weights_spread(0)
            expert_bias_tokens(0)

            def extras(n):
                if n == 2:
                    residual_transposes(0, 0)
                if n == 3:
                    residual_transposes(0, 1)
                if n == X1_UNIT:
                    for g in range(NK):
                        x_transposes(1, g)
                    logits(1)
                if n == X1_UNIT + 1:
                    weights_transposed(1)
                    weights_spread(1)
                    expert_bias_tokens(1)
                if n == RES1_UNIT:
                    residual_transposes(1, 0)
                if n == RES1_UNIT + 1:
                    residual_transposes(1, 1)

            for n in range(len(units) + 2):
                if n < len(units):
                    layer1(n)
                extras(n)
                if 1 <= n <= len(units):
                    layer2(n - 1)
                if n >= 2:
                    layer3(n - 2)


def lay_out(inp):
    import numpy as np

    f = np.float32
    where, n = columns()
    par = np.zeros((P, n), f)

    def put(name, a):
        a = np.asarray(a)
        a = a.reshape(a.shape[0], -1)
        lo, hi = where[name]
        par[0:a.shape[0], lo:hi] = a

    def twice(a):
        out = np.zeros((2 * a.shape[0], 2 * a.shape[1]), f)
        out[0:a.shape[0], 0:a.shape[1]] = a
        out[a.shape[0]:, a.shape[1]:] = a
        return out

    rows = np.arange(P)
    put("ident", np.eye(P, dtype=f))
    put("ones", np.ones((P, P), f))
    put("gn1", (rows[:, None] // 2 == rows[None, :] // 2) / f(2))
    put("gn2", (rows[:, None] // 4 == rows[None, :] // 4) / f(4))
    group3 = (rows % C) // (C // 2)
    put("gn3", (group3[:, None] == group3[None, :]) / f(C * WIN * 2))
    ch = np.arange(C)
    put("gna", (ch[:, None] // 8 == ch[None, :] // 8) / f(8 * WIN))
    put("w0", twice(inp["L0_conv_w0"][:, :, 0, 0].T))
    put("b0", np.concatenate([inp["L0_conv_b0"]] * 2)[:, None])
    w1 = inp["L0_conv_w1"]
    conv1 = np.zeros((2, C, TAPS, 2, C), f)
    per = w1.shape[1]
    for o in range(2 * C):
        g = o // (2 * C // 4)
        conv1[:, g * per:(g + 1) * per, :, o % 2, o // 2] = w1[o].reshape(per, TAPS)
    radix = lambda v: np.concatenate([v[0::2], v[1::2]])
    put("b1", radix(inp["L0_conv_b1"])[:, None])
    w2 = np.zeros((C, C), f)
    for o in range(C):
        g = o // (C // 2)
        w2[g * (C // 2):(g + 1) * (C // 2), o] = inp["L0_conv_w2"][o, :, 0, 0]
    put("w2", w2)
    put("b2", inp["L0_conv_b2"][:, None])
    w3 = np.zeros((C, 2, 2, C), f)
    b3 = np.zeros((2, C, 2), f)
    for o in range(2 * C):
        g, r, c = o // C, o % 2, o // 2
        w3[g * (C // 2):(g + 1) * (C // 2), 0, r, c] = inp["L0_conv_w3"][o, :, 0, 0]
        w3[g * (C // 2):(g + 1) * (C // 2), 1, 1 - r, c] = inp["L0_conv_w3"][o, :, 0, 0]
        b3[r, c, 0] = inp["L0_conv_b3"][o]
        b3[1 - r, c, 1] = inp["L0_conv_b3"][o]
    put("w3", w3)
    put("b3", b3.reshape(P, 2))
    put("weight", np.concatenate([inp["L0_conv_weight"]] * 2))
    put("fc", twice(inp["L1_attn_fc_w"].T))
    put("fcb", np.concatenate([inp["L1_attn_fc_b"]] * 2)[:, None])
    put("score", twice(inp["L1_attn_score_w"][:, None]))
    put("wr", np.concatenate([inp["L1_ffn_Wr"]] * 2))
    put("br", np.broadcast_to(inp["L1_ffn_br"], (P, E)))
    both = np.concatenate([inp["L1_ffn_W1"]] * 2, axis=1)
    put("ffn1", both.transpose(1, 0, 2))
    f2 = np.stack([twice(np.zeros((C, C), f))] * EP)
    for e in range(EP):
        f2[e, 0:C, 0:C] = inp["L1_ffn_W2"][2 * e]
        f2[e, C:, C:] = inp["L1_ffn_W2"][2 * e + 1]
    put("ffn2", f2.transpose(1, 0, 2))
    put("ffo", inp["L1_ffn_Wo"].reshape(EP, P, C).transpose(1, 0, 2))
    for i in (1, 2):
        names = [f"L1_ffn_{n}{i}" for n in ("b", "g", "be", "m", "v")]
        put(f"bn{i}", np.stack([inp[n].reshape(EP, P) for n in names]).transpose(2, 0, 1))
    emask = np.zeros((2, HID, EP, E), f)
    sel = np.zeros((E, EP, 2, HID), f)
    for e in range(E):
        emask[e % 2, :, e // 2, e] = 1
        sel[e, e // 2, e % 2, :] = 1
    put("emask", emask.reshape(P, -1))
    put("sel", sel)
    put("bo", inp["L1_ffn_bo"])
    return par, conv1.reshape(P, TAPS, P)


def kernel(**inputs):
    import numpy as np
    import concourse.bacc as bacc
    from concourse.bass_utils import run_bass_kernel_spmd

    inp = {name: np.asarray(a) for name, a in inputs.items()}
    par, conv1 = lay_out(inp)
    arrays = {"x": np.ascontiguousarray(inp["x"]), "params": par, "conv1_w": np.ascontiguousarray(conv1)}
    nc = bacc.Bacc("TRN2", target_bir_lowering=False, num_devices=1)
    aps = [nc.dram_tensor(n, a.shape, F32, kind="ExternalInput").ap() for n, a in arrays.items()]
    out = nc.dram_tensor("out", arrays["x"].shape, F32, kind="ExternalOutput").ap()
    conv_attention_experts(nc, *aps, out)
    r = run_bass_kernel_spmd(nc, [arrays], core_ids=[0])
    return r.results[0]["out"]
```

```python
from contextlib import ExitStack

import concourse.bass as bass
from concourse import mybir

ALU = mybir.AluOpType
ACT = mybir.ActivationFunctionType
F32 = mybir.dt.float32
F32R = mybir.dt.float32r
AX_X = mybir.AxisListType.X

P = 128
B, C, S = 16, 64, 16
PIX = S * S
PAIRS = B // 2
NK = 2
PK = PAIRS // NK
BK = B // NK
PAD = S + 2
TAPS = 9
WIN = 4
E, HID = 8, 64
EP = E // 2
Q = 2
EPS = 1e-5
BN_EPS = 1e-3
LOWEST = -3.0e38

COLS = dict(
    gn1=P, w0=P, b0=1, gn2=P, b1=1, ident=P, gn3=P, gna=C, w2=C, b2=1, w3=2 * P, b3=2, weight=C,
    fc=P, fcb=1, score=2, wr=Q * E, br=Q * E, ffn1=EP * P, ffn2=EP * P, ffo=EP * C,
    bn1=5 * EP, bn2=5 * EP, emask=EP * Q * E, ones=P,
)
ROW_COLS = dict(sel=Q * EP * P, bo=C, qmask=Q)


def columns(cols=COLS):
    at, out = 0, {}
    for name, n in cols.items():
        out[name] = (at, at + n)
        at += n
    return out, at


def conv_attention_experts(nc: bass.Bass, x: bass.AP, params: bass.AP, row_params: bass.AP, conv1_w: bass.AP, out: bass.AP):
    where, n_params = columns()
    row_where, n_rows = columns(ROW_COLS)
    n_early = where["b1"][1]
    x_pairs = x.rearrange("(b h) c y x -> b (h c) (y x)", h=2)
    out_pairs = out.rearrange("(b h) c y x -> b (h c) (y x)", h=2)

    with ExitStack() as ctx:
        def sb(name, shape, dt=F32):
            return ctx.enter_context(nc.sbuf_tensor(name, shape, dt))

        def sem(name):
            return ctx.enter_context(nc.semaphore(name))

        par = sb("par", [P, n_params])

        def w(name, rows=P):
            a, b = where[name]
            return par[0:rows, a:b]

        row_par = sb("row_par", [Q * E, n_rows])

        def r_(name):
            a, b = row_where[name]
            return row_par[:, a:b]

        xin = sb("xin", [P, PAIRS, PIX])
        xnorm = sb("xnorm", [P, PAIRS, PIX])
        act0 = sb("act0", [P, PAIRS, PIX])
        norm0 = sb("norm0", [P, PAIRS, PIX])
        pad = [sb(f"pad{h}", [P, PAIRS, PAD, PAD], F32R) for h in range(2)]
        y = sb("y", [P, B, PIX])
        x1 = sb("x1", [P, PAIRS, PIX])
        tok = sb("tok", [P, NK, Q, BK, C])
        square = sb("square", [P, NK, Q, BK, C])
        hn = sb("hn", [P, NK, Q, BK, C])
        ctxs = sb("ctxs", [P, NK, Q, C, BK])
        tok2 = sb("tok2", [P, NK, Q, BK, C])
        xs = sb("xs", [P, NK, Q, BK, P], F32R)
        h1 = [sb(f"h1_{i}", [P, 512]) for i in range(3)]
        h2 = [sb(f"h2_{i}", [P, 512]) for i in range(3)]

        def by_block(t, pattern, **sizes):
            return t[:].rearrange("p b n -> p (b n)").rearrange(pattern, k=NK, q=Q, **sizes)

        hch = by_block(xnorm, "p (k q n) -> p k q n")
        qch = by_block(act0, "p (k q n) -> p k q n")
        gated = by_block(norm0, "p (k q c t) -> p k q c t", c=C)
        tok2ch = by_block(x1, "p (k q b n) -> p k q b n", b=PK)
        decay = square[:].rearrange("p k q b c -> p (k q b c)").rearrange("p (k q c t) -> p k q c t", k=NK, q=Q, c=C)
        xn2 = hn
        res = act0
        held = [y[:, 2 * i:2 * i + 2, :].rearrange("p b n -> p (b n)") for i in range(8)]
        held += [t[:, 2 * i:2 * i + 2, :].rearrange("p b n -> p (b n)") for t in (xin, xnorm) for i in range(4)]

        w1raw = sb("w1raw", [P, TAPS, P])
        w1hi = sb("w1hi", [P, TAPS, P], F32R)
        w1lo = sb("w1lo", [P, TAPS, P], F32R)
        f1hi = sb("f1hi", [P, EP, P], F32R)
        f1lo = sb("f1lo", [P, EP, P], F32R)
        f2s = sb("f2s", [P, EP, P])
        w3d = sb("w3d", [C, P])
        b3d = sb("b3d", [P, 1])
        b2half = sb("b2half", [C, 1])
        expert_bias = sb("expert_bias", [Q * E, Q, 2, C])
        wb = sb("wb", [P, Q, EP, P])
        bias_ch = sb("bias_ch", [P, Q, P])
        minus_half = sb("minus_half", [P, 32])
        warm = sb("warm", [P, 512], mybir.dt.bfloat16)

        small_names = {}

        def tile(name, rows, *dims):
            n = 1
            for d in dims:
                n *= d
            if name not in small_names:
                small_names[name] = sb("s_" + name, [P, n])
            t = small_names[name][0:rows, 0:n]
            if len(dims) == 2:
                return t.rearrange("p (a b) -> p a b", a=dims[0])
            if len(dims) == 3:
                return t.rearrange("p (a b c) -> p a b c", a=dims[0], b=dims[1])
            return t

        bank = [ctx.enter_context(nc.psum_tensor(f"bank{i}", [P, 512], F32)) for i in range(8)]
        CONV0 = ((0, 1), (5, 6))
        CONV1 = (2, 3)
        CHAIN = ((5, 6), (0, 1))
        SMALL = 4
        TURN = 7
        Z1, Z2 = (2, 3), (5, 6)
        OUT = ((4, 7), (0, 1))

        def sem_list(*names):
            return [sem(n) for n in names]

        (early_params_loaded, params_loaded, conv1_w_loaded, rows_loaded, out_stored) = sem_list(
            "early_params_loaded", "params_loaded", "conv1_w_loaded", "rows_loaded", "out_stored")
        x_loaded = [sem(f"x_loaded_{k}") for k in range(NK)]
        vector_done = sem("vector_done")
        pool_done = sem("pool_done")
        small_ready = sem("small_ready")
        small_free = sem("small_free")
        var_ready = sem("var_ready")
        rstd_ready = sem("rstd_ready")
        stats_ready = sem("stats_ready")
        pads_zeroed, consts_ready, warm_ready = sem_list("pads_zeroed", "consts_ready", "warm_ready")
        w1_hi_ready, w1_split, f1_split = sem_list("w1_hi_ready", "w1_split", "f1_split")
        xnorm_ready, conv0_done, act0_ready, norm0_ready = sem_list("xnorm_ready", "conv0_done", "act0_ready", "norm0_ready")
        pad_hi_ready, pad_lo_ready, conv1_done, y_ready = sem_list("pad_hi_ready", "pad_lo_ready", "conv1_done", "y_ready")
        window_half_ready, window_tanh_ready = sem_list("window_half_ready", "window_tanh_ready")
        gn3_shift_ready, y_normalised, gated_y_ready = sem_list("gn3_shift_ready", "y_normalised", "gated_y_ready")
        outconv_done, gn4_shift_ready, x_shifted, x1_ready = sem_list("outconv_done", "gn4_shift_ready", "x_shifted", "x1_ready")
        tok_in_psum, tok_copied, square_ready, hn_ready = sem_list("tok_in_psum", "tok_copied", "square_ready", "hn_ready")
        hch_in_psum, hch_ready, fc_done, qch_ready = sem_list("hch_in_psum", "hch_ready", "fc_done", "qch_ready")
        exps_in, exps_ready, coef_ready, decay_ready = sem_list("exps_in", "exps_ready", "coef_ready", "decay_ready")
        tok2_ready, square2_ready, xn2_ready, xsum_ready = sem_list("tok2_ready", "square2_ready", "xn2_ready", "xsum_ready")
        xt_ready = sem("xt_ready")
        xs_hi, xs_ready = sem_list("xs_hi", "xs_ready")
        logits_in_psum, logits_ready, wexp_ready, wt_ready = sem_list("logits_in_psum", "logits_ready", "wexp_ready", "wt_ready")
        t2_in_psum, t2_copied, bias_ready, t2_biased = sem_list("t2_in_psum", "t2_copied", "bias_ready", "t2_biased")
        z1_done, h1_ready, z2_done = sem_list("z1_done", "h1_ready", "z2_done")
        z2_taken = sem("z2_taken")
        h2_ready = sem("h2_ready")
        held_ready = sem("held_ready")
        mlp_done0, mlp_done1, res_ready = sem_list("mlp_done0", "mlp_done1", "res_ready")

        ORDER = [("warm", 0), ("gn1", 0), ("gn1f", 0), ("gn1", 1), ("gn1f", 1), ("xnorm", 0), ("silu0", 0), ("xnorm", 1), ("gn2", 0), ("gn2f", 0),
                 ("silu0", 1), ("norm0", 0), ("conv", 0), ("gn2", 1), ("gn2f", 1), ("convb", 0), ("norm0", 1),
                 ("conv", 1), ("silu", 0), ("bn", 0), ("convb", 1), ("bnf", 0), ("ws", 0), ("conv", 2), ("silu", 1), ("s2row", 0),
                 ("ws", 1), ("convb", 2), ("ebias", 0), ("conv", 3), ("silu", 2), ("ws", 2), ("convb", 3),
                 ("conv", 4), ("silu", 3), ("ws", 3), ("gn3", 0), ("convb", 4), ("gn3f", 0), ("silu", 4), ("win", 0), ("conv", 5), ("w2", 0), ("ws", 4),
                 ("gna", 0), ("convb", 5), ("gnaf", 0), ("silu", 5), ("wan", 0), ("w3", 0), ("conv", 6), ("gate", 0),
                 ("outp", 0), ("convb", 6), ("ws", 5), ("gn4", 0), ("conv", 7), ("gn4f", 0), ("silu", 6), ("x1", 0), ("ws", 6), ("convb", 7), ("tok", 0),
                 ("ln1", 0), ("silu", 7), ("hn", 0), ("ws", 7), ("gn3", 1), ("gn3f", 1), ("hch", 0), ("win", 1), ("fc", 0),
                 ("w2", 1), ("score", 0), ("gna", 1), ("coef", 0), ("gnaf", 1), ("wan", 1), ("w3", 1), ("att", 0), ("gate", 1),
                 ("outp", 1), ("ln2", 0), ("gn4", 1), ("gn4f", 1), ("xn2", 0), ("x1", 1), ("xt", 0), ("tok", 1), ("ln1", 1),
                 ("unit", 0), ("hn", 1), ("unit", 1), ("hch", 1), ("unit", 2), ("fc", 1), ("unit", 3), ("score", 1), ("unit", 4),
                 ("unit", 5), ("coef", 1), ("unit", 6), ("unit", 7), ("att", 1), ("unit", 8), ("unit", 9), ("t2", 0), ("ln2", 1),
                 ("unit", 10), ("unit", 11), ("xn2", 1), ("unit", 12), ("unit", 13), ("unit", 14),
                 ("xt", 1), ("unit", 15), ("unit", 16), ("logits", 0), ("t2", 1),
                 ("wt", 0), ("wb", 0), ("wb", 1), ("bias", 0)]

        def positions(names):
            found = [s for s in ORDER if s[0] in names]
            return {s: i + 1 for i, s in enumerate(found)}

        SMALL_AT = positions({"gn1", "gn2", "s2row", "ebias", "gn3", "w2", "gna", "w3", "gn4", "score", "logits", "wt", "wb", "bias"})
        STATS_AT = positions({"gn1", "gn2", "gn3", "w2", "gna", "w3", "gn4", "s2row", "logits"})
        var_tiles, VAR_AT, at = {}, {}, 0
        for name, k in ORDER:
            parts = {"gn1f": [("gn1", P, PK)], "gn2f": [("gn2", P, PK)], "gn3f": [("gn3", P, BK)], "gnaf": [("gna", C, BK)],
                     "gn4f": [("gn4", P, PK)], "bn": [("bnv", P, 2 * EP)],
                     "ln1": [("ln1", P, BK), ("ln1q", P, BK)], "ln2": [("ln2", P, BK), ("ln2q", P, BK)]}.get(name, [])
            for part, rows, cols in parts:
                at += 1
                VAR_AT[part, k] = at
                var_tiles[part, k] = (f"{part}v{k}", rows, cols)

        def rstd(name):
            n, rows, cols = var_tiles[name]
            return tile(n + "r", rows, cols)

        def halves(k, q):
            return slice(k * PK, (k + 1) * PK), slice(q * P, (q + 1) * P)

        units = [(k, q, e, h) for k in range(NK) for q in range(Q) for e in range(EP) for h in range(2)]
        NU = len(units) // 2

        block = ctx.enter_context(nc.Block())

        @block.sync
        def _(sp):
            for b in range(PAIRS):
                sp.dma_start(xin[:, b, :], x_pairs[b]).then_inc(x_loaded[b // PK], 16)
            sp.dma_start(w1raw[:], conv1_w).then_inc(conv1_w_loaded, 16)
            for n in range(Q * NK):
                q, k = n // NK, n % NK
                pairs, pixels = halves(k, q)
                sp.wait_ge(res_ready, n + 1)
                sp.dma_start(out_pairs[pairs, :, pixels].rearrange("b p n -> p b n"),
                             res[:, pairs, pixels]).then_inc(out_stored, 16)
            sp.wait_ge(out_stored, 16 * Q * NK)

        @block.gpsimd
        def _(pool):
            G = nc.gpsimd
            steps = [0]

            def step(ins):
                steps[0] += 1
                ins.then_inc(pool_done, 1)
                pool.wait_ge(pool_done, steps[0])

            def power(name):
                n, rows, cols = var_tiles[name]
                pool.wait_ge(var_ready, VAR_AT[name])
                G.tensor_tensor(rstd(name), tile(n, rows, cols), minus_half[0:rows, 0:cols], ALU.pow).then_inc(rstd_ready, 1)

            def split_w1():
                pool.wait_ge(w1_hi_ready, 1)
                G.tensor_tensor(w1lo[:], w1raw[:], w1hi[:].bitcast(F32), ALU.subtract).then_inc(w1_split, 1)

            def normalise_y(k):
                pool.wait_ge(gn3_shift_ready, k + 1)
                r, nb = rstd(("gn3", k)), tile(f"gn3v{k}nb", P, BK)
                for b in range(BK):
                    img = y[:, k * BK + b, :]
                    G.tensor_scalar(img, img, r[:, b:b + 1], nb[:, b:b + 1], ALU.mult, ALU.add).then_inc(y_normalised, 1)

            def shift_x(k):
                pool.wait_ge(gn4_shift_ready, k + 1)
                nb = tile(f"gn4v{k}nb", P, PK)
                for i in range(PK):
                    img = xin[:, k * PK + i, :]
                    G.tensor_scalar(img, img, nb[:, i:i + 1], None, ALU.add).then_inc(x_shifted, 1)

            def sum_samples(k):
                pool.wait_ge(xn2_ready, Q * (k + 1))
                t = tile(f"xsum{k}", P, Q, 4, C)
                step(G.tensor_tensor(t, xn2[:, k, :, 0:4, :], xn2[:, k, :, 4:8, :], ALU.add))
                step(G.tensor_tensor(t[:, :, 0:2, :], t[:, :, 0:2, :], t[:, :, 2:4, :], ALU.add))
                step(G.tensor_tensor(t[:, :, 0, :], t[:, :, 0, :], t[:, :, 1, :], ALU.add))
                if k == NK - 1:
                    G.tensor_tensor(tile("xsum", P, Q, C), tile("xsum0", P, Q, 4, C)[:, :, 0, :], t[:, :, 0, :],
                                    ALU.add).then_inc(stats_ready, 1)

            def bias_residual():
                pool.wait_ge(bias_ready, 1)
                pool.wait_ge(t2_copied, Q * NK)
                for n in range(Q * NK):
                    q, k = n // NK, n % NK
                    G.tensor_tensor(tok2ch[:, k, q], tok2ch[:, k, q], bias_ch[:, q:q + 1, :].broadcast_to([P, PK, P]),
                                    ALU.add).then_inc(t2_biased, 1)

            G.memset(warm[:], 0.0).then_inc(warm_ready, 1)
            G.memset(minus_half[:], -0.5).then_inc(consts_ready, 1)
            for h in range(2):
                G.memset(pad[h][:].bitcast(F32), 0.0).then_inc(pads_zeroed, 1)
            pool.wait_ge(consts_ready, 1)
            for name, k in ORDER:
                if name == "gn1f":
                    power(("gn1", k))
                elif name == "xnorm" and k == 1:
                    split_w1()
                elif name == "bn":
                    power(("bnv", k))
                elif name in ("gn2f", "gn3f", "gnaf", "gn4f"):
                    power((name[:-1], k))
                elif name in ("ln1", "ln2"):
                    power((name, k))
                    power((name + "q", k))
                elif name == "win":
                    normalise_y(k)
                elif name == "x1":
                    shift_x(k)
                elif name == "xn2":
                    sum_samples(k)
                elif name == "bias":
                    bias_residual()

        @block.scalar
        def _(act):
            A = nc.scalar
            act.dma_start(par[:, 0:n_early], params[:, 0:n_early]).then_inc(early_params_loaded, 16)
            act.dma_start(par[:, n_early:], params[:, n_early:]).then_inc(params_loaded, 16)
            act.dma_start(row_par[:], row_params).then_inc(rows_loaded, 16)

            def silu0(k):
                for j in range(2):
                    act.wait_ge(conv0_done, 2 * k + j + 1)
                    b = k * PK + 2 * j
                    A.activation(act0[:, b:b + 2, :], bank[CONV0[k][j]][:].rearrange("p (b n) -> p b n", b=2),
                                 ACT.Silu, bias=w("b0")).then_inc(act0_ready, 1)
                if k == 0:
                    act.wait_ge(conv1_w_loaded, 16)
                    A.activation(w1hi[:], w1raw[:], ACT.Copy).then_inc(w1_hi_ready, 1)

            def pad_high(k):
                act.wait_ge(pads_zeroed, 2)
                for h in range(2):
                    own = slice(h * C, (h + 1) * C)
                    for j in range(2):
                        act.wait_ge(norm0_ready, 2 * k + j + 1)
                        pairs = slice(k * PK + 2 * j, k * PK + 2 * j + 2)
                        A.activation(pad[h][own, pairs, 1:S + 1, 1:S + 1],
                                     norm0[own, pairs, :].rearrange("p b (y x) -> p b y x", y=S),
                                     ACT.Copy).then_inc(pad_hi_ready, 1)

            def silu1(u):
                act.wait_ge(conv1_done, u + 1)
                k, j, h = u // 4, (u // 2) % 2, u % 2
                b = 2 * (k * PK + 2 * j) + h
                A.activation(y[:, b:b + 3:2, :], bank[CONV1[u % 2]][:].rearrange("p (b n) -> p b n", b=2),
                             ACT.Silu, bias=w("b1")).then_inc(y_ready, 1)

            def window_tanh(k):
                act.wait_ge(window_half_ready, k + 1)
                A.activation(tile(f"wth{k}", C, BK * WIN), tile(f"wh{k}", C, BK * WIN), ACT.Tanh).then_inc(window_tanh_ready, 1)

            def radix_tanh(k):
                act.wait_ge(small_ready, SMALL_AT["w3", k])
                A.activation(tile(f"wt{k}", P, BK * WIN), bank[SMALL][:, 0:BK * WIN], ACT.Tanh,
                             bias=b3d[:, 0:1], scale=0.5).then_inc(small_free, 1)

            def tok_copies(k):
                for q in range(Q):
                    act.wait_ge(tok_in_psum, Q * k + q + 1)
                    src = bank[CHAIN[k][q]][:].rearrange("p (b c) -> p b c", c=C)
                    A.activation(tok[:, k, q], src, ACT.Copy).then_inc(tok_copied, 1)
                    A.activation(square[:, k, q], src, ACT.Square).then_inc(square_ready, 1)

            def hch_copies(k):
                for q in range(Q):
                    act.wait_ge(hch_in_psum, Q * k + q + 1)
                    A.activation(hch[:, k, q, :], bank[CHAIN[k][q]][:], ACT.Copy).then_inc(hch_ready, 1)

            def fc_tanh(k):
                for q in range(Q):
                    act.wait_ge(fc_done, Q * k + q + 1)
                    A.activation(qch[:, k, q, :], bank[CHAIN[k][q]][:], ACT.Tanh, bias=w("fcb")).then_inc(qch_ready, 1)

            def attention_exps(k):
                act.wait_ge(exps_in, k + 1)
                A.activation(tile(f"aexp{k}", P, 2 * Q * BK), tile(f"aarg{k}", P, 2 * Q * BK), ACT.Exp).then_inc(exps_ready, 1)

            def spread_decay(k):
                act.wait_ge(coef_ready, k + 1)
                for q in range(Q):
                    A.activation(decay[:, k, q], tile(f"ascan{k}", P, Q, BK)[:, q:q + 1, :].broadcast_to([P, C, BK]),
                                 ACT.Copy).then_inc(decay_ready, 1)

            def squares2(k):
                for q in range(Q):
                    act.wait_ge(tok2_ready, Q * k + q + 1)
                    A.activation(square[:, k, q], tok2[:, k, q], ACT.Square).then_inc(square2_ready, 1)

            def high_x(k):
                for q in range(Q):
                    act.wait_ge(xt_ready, Q * k + q + 1)
                    for h in range(2):
                        own = slice(h * C, (h + 1) * C)
                        A.activation(xs[own, k, q, h::2, :], bank[CHAIN[k][q]][own, :].rearrange("p (b n) -> p b n", b=PK),
                                     ACT.Copy).then_inc(xs_hi, 1)

            def residual_copies(k):
                for q in range(Q):
                    act.wait_ge(t2_in_psum, Q * k + q + 1)
                    A.activation(tok2ch[:, k, q], bank[TURN][:].rearrange("p (b n) -> p b n", b=PK),
                                 ACT.Copy).then_inc(t2_copied, 1)

            def relu1(n):
                act.wait_ge(z1_done, n + 1)
                if n >= 3:
                    act.wait_ge(z2_done, n - 2)
                e = units[n][2]
                A.activation(h1[n % 3][:], bank[Z1[n % 2]][:], ACT.Relu, bias=tile("bnb", P, 2 * EP)[:, e:e + 1],
                             scale=tile("bns", P, 2 * EP)[:, e:e + 1]).then_inc(h1_ready, 1)

            def relu2(n):
                act.wait_ge(z2_done, n + 1)
                e = units[n][2]
                A.activation(held[n], bank[Z2[n % 2]][:], ACT.Relu,
                             bias=tile("bnb", P, 2 * EP)[:, EP + e:EP + e + 1]).then_inc(z2_taken, 1)

            def route():
                act.wait_ge(logits_ready, 1)
                A.activation(tile("wexp", P, Q * E), tile("lg", P, Q * E), ACT.Exp).then_inc(wexp_ready, 1)

            def weights_copy(q):
                act.wait_ge(small_ready, SMALL_AT["wb", q])
                A.activation(wb[:, q], bank[SMALL][:].rearrange("p (e n) -> p e n", e=EP), ACT.Copy).then_inc(small_free, 1)

            def unit(n):
                relu1(n)
                if 1 <= n <= NU:
                    relu2(n - 1)

            stages = {"silu0": silu0, "norm0": pad_high, "silu": silu1, "w2": window_tanh, "w3": radix_tanh, "tok": tok_copies,
                      "hch": hch_copies, "fc": fc_tanh, "coef": attention_exps, "att": lambda k: (spread_decay(k), squares2(k)),
                      "xt": high_x, "t2": residual_copies, "unit": unit, "wb": weights_copy}
            act.wait_ge(early_params_loaded, 16)
            for name, k in ORDER:
                if name in stages:
                    stages[name](k)
                elif name == "logits":
                    route()
            for n in range(NU + 1, len(units)):
                relu1(n)

        @block.vector
        def _(dve):
            steps = [0]

            def step(ins):
                steps[0] += 1
                ins.then_inc(vector_done, 1)
                dve.wait_ge(vector_done, steps[0])

            V = nc.vector

            def each(t, rows, n, width):
                return t.rearrange("p (b o) -> p b o", o=1).broadcast_to([rows, n, width])

            def group_finish(name, n, rows=P):
                t, _, _ = var_tiles[name]
                ms, sq = tile(t + "ms", rows, 2, n), tile(t + "sq", rows, n)
                dve.wait_ge(small_ready, SMALL_AT[name])
                V.tensor_copy(ms, bank[SMALL][0:rows, 0:2 * n].rearrange("p (a n) -> p a n", a=2)).then_inc(small_free, 1)
                dve.wait_ge(small_free, SMALL_AT[name])
                step(V.tensor_tensor(sq, ms[:, 0, :], ms[:, 0, :], ALU.mult))
                V.scalar_tensor_tensor(tile(t, rows, n), ms[:, 1, :], EPS, sq, ALU.add, ALU.subtract).then_inc(var_ready, 1)

            def group_shift(name, n, rows=P, signal=None):
                t, _, _ = var_tiles[name]
                dve.wait_ge(rstd_ready, VAR_AT[name])
                ins = V.scalar_tensor_tensor(tile(t + "nb", rows, n), tile(t + "ms", rows, 2, n)[:, 0, :], -1.0, rstd(name),
                                             ALU.mult, ALU.mult)
                if signal is None:
                    step(ins)
                else:
                    ins.then_inc(signal, 1)
                    dve.wait_ge(signal, name[1] + 1)
                return rstd(name), tile(t + "nb", rows, n)

            def channel_stats(name, source, n, arrived=None):
                t, _, _ = var_tiles[name]
                raw, mv, e2 = tile(t + "raw", P, n, 6), tile(t + "mv", P, n, 2), tile(t + "e2", P, 2, n)
                for i in range(n):
                    if arrived is not None:
                        arrived(i)
                    ins = V.bn_stats(raw[:, i, :], source(i))
                step(ins)
                for i in range(n):
                    ins = V.bn_aggr(mv[:, i, :], raw[:, i, :])
                step(ins)
                V.tensor_copy(e2[:, 0, :], mv[:, :, 0])
                step(V.tensor_tensor(e2[:, 1, :], mv[:, :, 0], mv[:, :, 0], ALU.mult))
                V.tensor_tensor(e2[:, 1, :], e2[:, 1, :], mv[:, :, 1], ALU.add).then_inc(stats_ready, 1)

            def gn1_stats(k):
                dve.wait_ge(x_loaded[k], 16 * PK)
                channel_stats(("gn1", k), lambda i: xin[:, k * PK + i, :], PK)

            def normalise_x(k):
                r, nb = group_shift(("gn1", k), PK)
                for i in range(PK):
                    V.tensor_scalar(xnorm[:, k * PK + i, :], xin[:, k * PK + i, :], r[:, i:i + 1], nb[:, i:i + 1],
                                    ALU.mult, ALU.add).then_inc(xnorm_ready, 1)

            def gn2_stats(k):
                channel_stats(("gn2", k), lambda i: act0[:, k * PK + i, :], PK,
                              lambda i: dve.wait_ge(act0_ready, 2 * k + i // 2 + 1))

            def normalise_0(k):
                r, nb = group_shift(("gn2", k), PK)
                for i in range(PK):
                    ins = V.tensor_scalar(norm0[:, k * PK + i, :], act0[:, k * PK + i, :], r[:, i:i + 1], nb[:, i:i + 1],
                                          ALU.mult, ALU.add)
                    if i % 2:
                        ins.then_inc(norm0_ready, 1)
                dve.wait_ge(norm0_ready, 2 * k + 2)
                for h in range(2):
                    own, other = slice(h * C, (h + 1) * C), slice((1 - h) * C, (2 - h) * C)
                    for j in range(2):
                        dve.wait_ge(pad_hi_ready, 4 * k + 2 * h + j + 1)
                        pairs = slice(k * PK + 2 * j, k * PK + 2 * j + 2)
                        V.tensor_tensor(pad[h][other, pairs, 1:S + 1, 1:S + 1],
                                        norm0[own, pairs, :].rearrange("p b (y x) -> p b y x", y=S),
                                        pad[h][own, pairs, 1:S + 1, 1:S + 1].bitcast(F32), ALU.subtract).then_inc(pad_lo_ready, 1)

            def batch_norm_variances():
                dve.wait_ge(params_loaded, 16)
                bn1, bn2 = (w(n).rearrange("p (a e) -> p a e", a=5) for n in ("bn1", "bn2"))
                bnvar = tile("bnvv0", P, 2 * EP)
                V.tensor_scalar(bnvar[:, 0:EP], bn1[:, 4, :], BN_EPS, None, ALU.add)
                V.tensor_scalar(bnvar[:, EP:2 * EP], bn2[:, 4, :], BN_EPS, None, ALU.add).then_inc(var_ready, 1)

            def fold_weights():
                bn1, bn2 = (w(n).rearrange("p (a e) -> p a e", a=5) for n in ("bn1", "bn2"))
                bns, bnb = tile("bns", P, 2 * EP), tile("bnb", P, 2 * EP)
                dve.wait_ge(rstd_ready, VAR_AT["bnv", 0])
                r = rstd(("bnv", 0))
                V.tensor_tensor(bns[:, 0:EP], bn1[:, 1, :], r[:, 0:EP], ALU.mult)
                V.tensor_tensor(bns[:, EP:2 * EP], bn2[:, 1, :], r[:, EP:2 * EP], ALU.mult)
                V.tensor_tensor(bnb[:, 0:EP], bn1[:, 0, :], bn1[:, 3, :], ALU.subtract)
                step(V.tensor_tensor(bnb[:, EP:2 * EP], bn2[:, 0, :], bn2[:, 3, :], ALU.subtract))
                step(V.tensor_tensor(bnb, bnb, bns, ALU.mult))
                V.tensor_tensor(bnb[:, 0:EP], bnb[:, 0:EP], bn1[:, 2, :], ALU.add)
                step(V.tensor_tensor(bnb[:, EP:2 * EP], bnb[:, EP:2 * EP], bn2[:, 2, :], ALU.add))
                diag = tile("diag", P, EP, P)
                for e in range(EP):
                    V.tensor_scalar(diag[:, e, :], w("ident"), bns[:, EP + e:EP + e + 1], None, ALU.mult)
                V.tensor_tensor(tile("bcol", P, EP, Q * E), w("emask").rearrange("p (e m) -> p e m", e=EP),
                                each(bnb[:, EP:2 * EP], P, EP, Q * E), ALU.mult)
                V.tensor_scalar(tile("negb", P, EP), bnb[:, EP:2 * EP], -1.0, None, ALU.mult)
                V.tensor_scalar(b2half[:], w("b2", C), 0.5, None, ALU.mult)
                V.tensor_tensor(w3d[:], w("w3", C)[:, 0:P], w("w3", C)[:, P:2 * P], ALU.subtract)
                step(V.tensor_tensor(b3d[:], w("b3")[:, 0:1], w("b3")[:, 1:2], ALU.subtract))
                V.tensor_scalar(b3d[:], b3d[:], 0.5, None, ALU.mult).then_inc(stats_ready, 1)

            def scale_second_layer():
                dve.wait_ge(small_ready, SMALL_AT["s2row", 0])
                V.tensor_tensor(f2s[:], w("ffn2").rearrange("p (e m) -> p e m", e=EP),
                                bank[SMALL][:].rearrange("p (e m) -> p e m", e=EP), ALU.mult).then_inc(small_free, 1)
                f1 = w("ffn1").rearrange("p (e m) -> p e m", e=EP)
                step(V.tensor_copy(f1hi[:], f1))
                V.tensor_tensor(f1lo[:], f1, f1hi[:].bitcast(F32), ALU.subtract).then_inc(f1_split, 1)

            def spread_expert_bias():
                dve.wait_ge(rows_loaded, 16)
                dve.wait_ge(small_ready, SMALL_AT["ebias", 0])
                src = bank[SMALL][0:Q * E, 0:C].rearrange("p (o c) -> p o c", o=1).broadcast_to([Q * E, 2, C])
                V.tensor_scalar(expert_bias[:, 0], src, r_("qmask")[:, 0:1], None, ALU.mult)
                V.tensor_scalar(expert_bias[:, 1], src, r_("qmask")[:, 1:2], None, ALU.mult).then_inc(small_free, 1)

            def window_stats(u):
                dve.wait_ge(y_ready, u + 1)
                k, j, h = u // 4, (u // 2) % 2, u % 2
                ws = tile(f"ws{k}", P, BK * WIN, 6)
                for i in range(2):
                    b = 2 * (2 * j + i) + h
                    img = y[:, k * BK + b, :].rearrange("p (a y c x) -> p a y c x", a=2, y=8, c=2)
                    for n in range(WIN):
                        ins = V.bn_stats(ws[:, b * WIN + n, :], img[:, n // 2, :, n % 2, :])
                step(ins)

            def gn3_stats(k):
                n = BK * WIN
                ws = tile(f"ws{k}", P, n, 6)
                st, sq, sm = tile(f"wst{k}", P, 2, n), tile(f"wsq{k}", P, n, 2), tile(f"wsm{k}", P, 2, n)
                means = ws.rearrange("p n (a t) -> p n a t", a=2)[:, :, :, 1]
                V.tensor_tensor(sq, means, means, ALU.mult)
                V.tensor_tensor(st[:, 0, :], ws[:, :, 1], ws[:, :, 4], ALU.add)
                step(V.tensor_tensor(sm[:, 0, :], ws[:, :, 2], ws[:, :, 5], ALU.add))
                step(V.tensor_tensor(sm[:, 1, :], sq[:, :, 0], sq[:, :, 1], ALU.add))
                step(V.scalar_tensor_tensor(st[:, 1, :], sm[:, 0, :], 1.0 / 32, sm[:, 1, :], ALU.mult, ALU.add))
                V.tensor_reduce(tile(f"wsum{k}", P, 2 * BK), st.rearrange("p a (b n) -> p (a b) n", n=WIN), AX_X,
                                ALU.add).then_inc(stats_ready, 1)

            def window_in(k):
                r, nb = group_shift(("gn3", k), BK, signal=gn3_shift_ready)
                st = tile(f"wst{k}", P, 2, BK * WIN)
                a = tile(f"win{k}", P, BK, WIN)
                step(V.scalar_tensor_tensor(a, st[:, 0, :].rearrange("p (b n) -> p b n", n=WIN), 0.5, each(r, P, BK, WIN),
                                            ALU.mult, ALU.mult))
                step(V.tensor_tensor(a, a, each(nb, P, BK, WIN), ALU.add))
                other = tile(f"wino{k}", C, BK, WIN)
                step(V.tensor_copy(other, a[C:P]))
                V.tensor_tensor(tile(f"wmax{k}", C, BK, WIN), a[0:C], other, ALU.max).then_inc(stats_ready, 1)

            def window_half(k):
                dve.wait_ge(small_ready, SMALL_AT["w2", k])
                V.tensor_scalar(tile(f"wh{k}", C, BK * WIN), bank[SMALL][0:C, 0:BK * WIN], 0.5, b2half[:, 0:1],
                                ALU.mult, ALU.add).then_inc(window_half_ready, 1)
                dve.wait_ge(window_half_ready, k + 1)
                V.tensor_copy(tile(f"wfree{k}", C, 1), tile(f"wh{k}", C, BK * WIN)[:, 0:1]).then_inc(small_free, 1)

            def window_norm_stats(k):
                wa = tile(f"wa{k}", C, 2, BK * WIN)
                dve.wait_ge(window_tanh_ready, k + 1)
                step(V.scalar_tensor_tensor(wa[:, 0, :], tile(f"wth{k}", C, BK * WIN), 1.0, tile(f"wh{k}", C, BK * WIN),
                                            ALU.add, ALU.mult))
                step(V.tensor_tensor(wa[:, 1, :], wa[:, 0, :], wa[:, 0, :], ALU.mult))
                V.tensor_reduce(tile(f"wr{k}", C, 2 * BK), wa.rearrange("p a (b n) -> p (a b) n", n=WIN), AX_X,
                                ALU.add).then_inc(stats_ready, 1)

            def window_normalise(k):
                r, nb = group_shift(("gna", k), BK, C)
                a = tile(f"wa{k}", C, 2, BK * WIN)[:, 0, :].rearrange("p (b n) -> p b n", n=WIN)
                an = tile(f"wan{k}", C, BK, WIN)
                step(V.tensor_tensor(an, a, each(r, C, BK, WIN), ALU.mult))
                V.tensor_tensor(an, an, each(nb, C, BK, WIN), ALU.add).then_inc(stats_ready, 1)

            def gate_y(k):
                dve.wait_ge(small_free, SMALL_AT["w3", k])
                g = tile(f"gate{k}", P, BK * 2, S)
                step(V.tensor_scalar(g.rearrange("p n (c x) -> p (n c) x", c=2), each(tile(f"wt{k}", P, BK * WIN), P, BK * WIN, 8),
                                     0.5, 0.5, ALU.mult, ALU.add))
                for j in range(2):
                    dve.wait_ge(y_normalised, BK * k + 4 * j + 4)
                    yk = y[:, k * BK + 4 * j:k * BK + 4 * j + 4, :].rearrange("p b (a y x) -> p (b a) y x", a=2, y=8)
                    gj = g[:, 8 * j:8 * j + 8, :]
                    V.tensor_tensor(yk, yk, gj.rearrange("p n (o x) -> p n o x", o=1).broadcast_to([P, BK, 8, S]),
                                    ALU.mult).then_inc(gated_y_ready, 1)

            def image(k, i):
                return bank[CHAIN[k][i // 2]][:, (i % 2) * PIX:(i % 2 + 1) * PIX]

            def gn4_stats(k):
                channel_stats(("gn4", k), lambda i: image(k, i), PK, lambda i: dve.wait_ge(outconv_done, 2 * k + i // 2 + 1))

            def residual1(k):
                r, _ = group_shift(("gn4", k), PK, signal=gn4_shift_ready)
                for i in range(PK):
                    dve.wait_ge(x_shifted, PK * k + i + 1)
                    V.scalar_tensor_tensor(x1[:, k * PK + i, :], image(k, i), r[:, i:i + 1], xin[:, k * PK + i, :],
                                           ALU.mult, ALU.add).then_inc(x1_ready, 1)

            def layer_norm_stats(name, k, source):
                n = Q * BK
                s, m = tile(f"{name}s{k}", P, 2, n), tile(f"{name}m{k}", P, n)
                V.tensor_reduce(s[:, 0, :].rearrange("p (q b) -> p q b", q=Q), source[:, k], AX_X, ALU.add)
                for q in range(Q):
                    dve.wait_ge(square_ready if name == "ln1" else square2_ready, Q * k + q + 1)
                step(V.tensor_reduce(s[:, 1, :].rearrange("p (q b) -> p q b", q=Q), square[:, k], AX_X, ALU.add))
                step(V.tensor_scalar(s, s, 1.0 / C, None, ALU.mult))
                step(V.tensor_tensor(m, s[:, 0, :], s[:, 0, :], ALU.mult))
                for q, part in enumerate((name, name + "q")):
                    t, _, _ = var_tiles[part, k]
                    cols = slice(q * BK, (q + 1) * BK)
                    V.scalar_tensor_tensor(tile(t, P, BK), s[:, 1, cols], EPS, m[:, cols], ALU.add,
                                           ALU.subtract).then_inc(var_ready, 1)
                means = s[:, 0, :].rearrange("p (q b o) -> p q b o", q=Q, o=1)
                for q in range(Q):
                    ins = V.tensor_tensor(hn[:, k, q], source[:, k, q], means[:, q].broadcast_to([P, BK, C]), ALU.subtract)
                step(ins)

            def layer_norm_scale(name, k, ready):
                for q, part in enumerate((name, name + "q")):
                    dve.wait_ge(rstd_ready, VAR_AT[part, k])
                    V.tensor_tensor(hn[:, k, q], hn[:, k, q], each(rstd((part, k)), P, BK, C), ALU.mult).then_inc(ready, 1)

            def ln1_stats(k):
                dve.wait_ge(tok_copied, Q * (k + 1))
                layer_norm_stats("ln1", k, tok)

            scores = tile("scores", P, Q, B)
            runmax, runsum = tile("runmax", P, Q, B + 1), tile("runsum", P, Q, B + 1)

            def attention_coefficients(k):
                t0, t1 = k * BK, (k + 1) * BK
                dve.wait_ge(small_ready, SMALL_AT["score", k])
                if k == 0:
                    V.memset(runmax[:, :, 0:1], LOWEST)
                    V.memset(runsum[:, :, 0:1], 0.0)
                V.tensor_copy(scores[:, :, t0:t1], bank[SMALL][:, 0:Q * BK].rearrange("p (q b) -> p q b", q=Q)).then_inc(small_free, 1)
                dve.wait_ge(small_free, SMALL_AT["score", k])
                for q in range(Q):
                    e = scores[:, q, t0:t1]
                    ins = V.tensor_tensor_scan(runmax[:, q, t0 + 1:t1 + 1], e, e, runmax[:, q, t0:t0 + 1], ALU.max, ALU.max)
                step(ins)
                arg = tile(f"aarg{k}", P, 2, Q, BK)
                V.tensor_tensor(arg[:, 0], runmax[:, :, t0:t1], runmax[:, :, t0 + 1:t1 + 1], ALU.subtract)
                V.tensor_tensor(arg[:, 1], scores[:, :, t0:t1], runmax[:, :, t0 + 1:t1 + 1], ALU.subtract).then_inc(exps_in, 1)

            def attend(k):
                t0, t1 = k * BK, (k + 1) * BK
                dve.wait_ge(exps_ready, k + 1)
                ex = tile(f"aexp{k}", P, 2, Q, BK)
                inv, b_, a_ = tile(f"inv{k}", P, Q, BK), tile(f"coefb{k}", P, Q, BK), tile(f"coefa{k}", P, Q, BK)
                ascan = tile(f"ascan{k}", P, Q, BK)
                V.memset(ascan[:, :, 0:1], 0.0)
                for q in range(Q):
                    ins = V.tensor_tensor_scan(runsum[:, q, t0 + 1:t1 + 1], ex[:, 0, q, :], ex[:, 1, q, :], runsum[:, q, t0:t0 + 1],
                                               ALU.mult, ALU.add)
                step(ins)
                V.tensor_tensor(a_, ex[:, 0], runsum[:, :, t0:t1], ALU.mult)
                step(V.reciprocal(inv, runsum[:, :, t0 + 1:t1 + 1]))
                V.tensor_tensor(b_, ex[:, 1], inv, ALU.mult)
                step(V.tensor_tensor(a_, a_, inv, ALU.mult))
                V.tensor_copy(ascan[:, :, 1:], a_[:, :, 1:]).then_inc(coef_ready, 1)
                for q in range(Q):
                    ins = V.tensor_tensor(gated[:, k, q], hn[:, k, q].rearrange("p b c -> p c b"),
                                          b_[:, q:q + 1, :].broadcast_to([P, C, BK]), ALU.mult)
                step(ins)
                if k:
                    for q in range(Q):
                        ins = V.scalar_tensor_tensor(gated[:, k, q, :, 0], ctxs[:, k - 1, q, :, BK - 1], a_[:, q, 0:1],
                                                     gated[:, k, q, :, 0], ALU.mult, ALU.add)
                    step(ins)
                for q in range(Q):
                    flat = lambda t: t[:, k, q].rearrange("p c b -> p (c b)")
                    dve.wait_ge(decay_ready, Q * k + q + 1)
                    step(V.tensor_tensor_scan(flat(ctxs), flat(decay), flat(gated), 0.0, ALU.mult, ALU.add))
                    V.tensor_tensor(tok2[:, k, q], tok[:, k, q], ctxs[:, k, q].rearrange("p c b -> p b c"), ALU.add).then_inc(tok2_ready, 1)

            def ln2_stats(k):
                dve.wait_ge(tok2_ready, Q * (k + 1))
                layer_norm_stats("ln2", k, tok2)

            def low_x(k):
                for q in range(Q):
                    dve.wait_ge(xs_hi, 2 * (Q * k + q) + 2)
                    for h in range(2):
                        own, other = slice(h * C, (h + 1) * C), slice((1 - h) * C, (2 - h) * C)
                        V.tensor_tensor(xs[other, k, q, h::2, :], bank[CHAIN[k][q]][own, :].rearrange("p (b n) -> p b n", b=PK),
                                        xs[own, k, q, h::2, :].bitcast(F32), ALU.subtract).then_inc(xs_ready, 1)

            def turned_sum():
                dve.wait_ge(small_ready, SMALL_AT["logits", 0] )
                V.tensor_copy(tile("xsumT", P, P), bank[SMALL][:, 0:P]).then_inc(xsum_ready, 1)
                dve.wait_ge(logits_in_psum, 1)
                lg, mx = tile("lg", P, Q, E), tile("lmax", P, Q)
                V.scalar_tensor_tensor(lg, bank[SMALL][:, 0:Q * E].rearrange("p (q e) -> p q e", q=Q), 1.0 / B,
                                       w("br").rearrange("p (q e) -> p q e", q=Q), ALU.mult, ALU.add).then_inc(small_free, 1)
                dve.wait_ge(small_free, SMALL_AT["logits", 0])
                step(V.tensor_reduce(mx, lg, AX_X, ALU.max))
                V.tensor_tensor(lg, lg, each(mx, P, Q, E), ALU.subtract).then_inc(logits_ready, 1)
                ex, sm = tile("wexp", P, Q, E), tile("wsum", P, Q)
                dve.wait_ge(wexp_ready, 1)
                step(V.tensor_reduce(sm, ex, AX_X, ALU.add))
                step(V.reciprocal(sm, sm))
                V.tensor_tensor(tile("wsoft", P, Q, E), ex, each(sm, P, Q, E), ALU.mult).then_inc(wt_ready, 1)

            def weights_turned():
                dve.wait_ge(small_ready, SMALL_AT["wt", 0])
                V.tensor_copy(tile("wT", Q * E, P), bank[SMALL][0:Q * E, 0:P]).then_inc(small_free, 1)

            def bias_taken():
                dve.wait_ge(small_ready, SMALL_AT["bias", 0])
                V.tensor_copy(bias_ch[:], bank[SMALL][:, 0:Q * P].rearrange("p (q n) -> p q n", q=Q)).then_inc(bias_ready, 1)

            def weigh(n):
                k, q, e, h = units[n]
                m = n - NU
                dve.wait_ge(z2_done, n + 1)
                if m >= 3:
                    dve.wait_ge(mlp_done1, m - 2)
                V.scalar_tensor_tensor(h2[m % 3][:].rearrange("p (b n) -> p b n", b=PK),
                                       bank[Z2[n % 2]][:].rearrange("p (b n) -> p b n", b=PK), tile("negb", P, EP)[:, e:e + 1],
                                       wb[:, q, e:e + 1, :].broadcast_to([P, PK, P]), ALU.max, ALU.mult).then_inc(h2_ready, 1)

            def weigh_held(n):
                k, q, e, h = units[n]
                t = held[n].rearrange("p (b n) -> p b n", b=PK)
                V.scalar_tensor_tensor(t, t, tile("negb", P, EP)[:, e:e + 1], wb[:, q, e:e + 1, :].broadcast_to([P, PK, P]),
                                       ALU.add, ALU.mult).then_inc(held_ready, 1)

            def finish(k, q):
                dve.wait_ge((mlp_done0, mlp_done1)[k], 8 * (q + 1))
                dve.wait_ge(t2_biased, q * NK + k + 1)
                pairs, pixels = halves(k, q)
                V.tensor_tensor(res[:, pairs, pixels], bank[OUT[k][q]][:].rearrange("p (b n) -> p b n", b=PK),
                                tok2ch[:, k, q], ALU.add).then_inc(res_ready, 1)

            stages = {
                "gn1": gn1_stats, "gn1f": lambda k: group_finish(("gn1", k), PK), "xnorm": normalise_x,
                "gn2": gn2_stats, "gn2f": lambda k: group_finish(("gn2", k), PK), "norm0": normalise_0,
                "bn": lambda k: batch_norm_variances(), "bnf": lambda k: fold_weights(),
                "s2row": lambda k: scale_second_layer(), "ebias": lambda k: spread_expert_bias(),
                "ws": window_stats, "gn3": gn3_stats, "gn3f": lambda k: group_finish(("gn3", k), BK), "win": window_in,
                "w2": window_half, "gna": window_norm_stats, "gnaf": lambda k: group_finish(("gna", k), BK, C),
                "wan": window_normalise, "gate": gate_y, "gn4": gn4_stats, "gn4f": lambda k: group_finish(("gn4", k), PK),
                "x1": residual1, "ln1": ln1_stats, "hn": lambda k: layer_norm_scale("ln1", k, hn_ready),
                "coef": attention_coefficients, "att": attend, "ln2": ln2_stats,
                "xn2": lambda k: layer_norm_scale("ln2", k, xn2_ready), "xt": low_x, "logits": lambda k: turned_sum(),
                "wt": lambda k: weights_turned(), "bias": lambda k: bias_taken(),
            }
            for name, k in ORDER:
                if name in stages:
                    stages[name](k)
            dve.wait_ge(small_free, SMALL_AT["wb", 1])
            for m in range(NU):
                weigh(NU + m)
                weigh_held(m)
                if m == NU // 2 + 3:
                    finish(0, 0)
                    finish(1, 0)
            finish(0, 1)
            finish(1, 1)

        @block.tensor
        def _(pe):
            T = nc.tensor

            def small(name):
                if SMALL_AT[name] > 1:
                    pe.wait_ge(small_free, SMALL_AT[name] - 1)

            def group_product(name, matrix, rhs, rows, n):
                small(name)
                pe.wait_ge(stats_ready, STATS_AT[name])
                T.matmul(bank[SMALL][0:rows, 0:n], matrix, rhs, start=True, stop=True).then_inc(small_ready, 1)

            def warm_up():
                pe.wait_ge(warm_ready, 1)
                for _ in range(14):
                    T.matmul(bank[TURN][:], warm[:, 0:P], warm[:], start=True, stop=True)
                pe.wait_ge(early_params_loaded, 16)

            def conv0(k):
                for j in range(PK // 2):
                    b = k * PK + 2 * j
                    pe.wait_ge(xnorm_ready, b + 2)
                    T.matmul(bank[CONV0[k][j]][:], w("w0"), xnorm[:, b:b + 2, :], start=True, stop=True).then_inc(conv0_done, 1)

            def second_scale_row():
                small(("s2row", 0))
                pe.wait_ge(params_loaded, 16)
                pe.wait_ge(stats_ready, STATS_AT["s2row", 0])
                T.matmul(bank[SMALL][:], w("ones"), tile("diag", P, EP * P), start=True, stop=True).then_inc(small_ready, 1)

            wo = w("ffo").rearrange("p (e m) -> p e m", e=EP)

            def expert_biases():
                small(("ebias", 0))
                pe.wait_ge(rows_loaded, 16)
                for e in range(EP):
                    T.matmul(bank[SMALL][0:Q * E, 0:C], tile("bcol", P, EP, Q * E)[:, e, :], wo[:, e, :], start=(e == 0), stop=False)
                T.matmul(bank[SMALL][0:Q * E, 0:C], w("ident", Q * E)[:, 0:Q * E], r_("bo"), start=False, stop=True).then_inc(small_ready, 1)

            def conv1(u, part):
                k, j, h = u // 4, (u // 2) % 2, u % 2
                if part == 0:
                    if u == 0:
                        pe.wait_ge(w1_split, 1)
                    pe.wait_ge(pad_lo_ready, 4 * k + 2 * h + j + 1)
                    if u >= 2:
                        pe.wait_ge(y_ready, u - 1)
                b = k * PK + 2 * j
                for tap in (range(0, 5) if part == 0 else range(5, TAPS)):
                    dy, dx = tap // 3, tap % 3
                    for weights in (w1hi, w1lo):
                        ins = T.matmul(bank[CONV1[u % 2]][:], weights[:, tap, :], pad[h][:, b:b + 2, dy:dy + S, dx:dx + S],
                                       start=(tap == 0 and weights is w1hi), stop=(tap == TAPS - 1 and weights is w1lo))
                if part == 1:
                    ins.then_inc(conv1_done, 1)

            def out_product(k):
                if k == 0:
                    pe.wait_ge(act0_ready, 4)
                for j in range(2):
                    pe.wait_ge(gated_y_ready, 2 * k + j + 1)
                    b = k * BK + 4 * j
                    for h in range(2):
                        ins = T.matmul(bank[CHAIN[k][j]][h * C:(h + 1) * C, :], w("weight"), y[:, b + h:b + h + 3:2, :], start=True, stop=True)
                    ins.then_inc(outconv_done, 1)

            def to_tokens(k):
                pe.wait_ge(x1_ready, PK * (k + 1))
                for q in range(Q):
                    for i in range(PK):
                        ins = T.transpose(bank[CHAIN[k][q]][:, i * P:(i + 1) * P], x1[:, k * PK + i, q * P:(q + 1) * P], w("ident"))
                    ins.then_inc(tok_in_psum, 1)

            def pair_of(t, k, q, i):
                return t[:, k, q, 2 * i:2 * i + 2, :].rearrange("p b c -> p (b c)")

            def to_channels(k):
                pe.wait_ge(square_ready, Q * (k + 1))
                for q in range(Q):
                    pe.wait_ge(hn_ready, Q * k + q + 1)
                    for i in range(PK):
                        ins = T.transpose(bank[CHAIN[k][q]][:, i * P:(i + 1) * P], pair_of(hn, k, q, i), w("ident"))
                    ins.then_inc(hch_in_psum, 1)

            def fc(k):
                for q in range(Q):
                    pe.wait_ge(hch_ready, Q * k + q + 1)
                    T.matmul(bank[CHAIN[k][q]][:], w("fc"), hch[:, k, q, :], start=True, stop=True).then_inc(fc_done, 1)

            def score(k):
                small(("score", k))
                for q in range(Q):
                    pe.wait_ge(qch_ready, Q * k + q + 1)
                    for i in range(PK):
                        at = q * BK + 2 * i
                        ins = T.matmul(bank[SMALL][:, at:at + 2], qch[:, k, q, i * P:(i + 1) * P], w("score"), start=True, stop=True)
                ins.then_inc(small_ready, 1)

            def x_transposes(k):
                pe.wait_ge(qch_ready, Q * (k + 1))
                for q in range(Q):
                    pe.wait_ge(xn2_ready, Q * k + q + 1)
                    for i in range(PK):
                        ins = T.transpose(bank[CHAIN[k][q]][:, i * P:(i + 1) * P], pair_of(xn2, k, q, i), w("ident"))
                    ins.then_inc(xt_ready, 1)

            def residual_transposes(k):
                for q in range(Q):
                    if Q * k + q:
                        pe.wait_ge(t2_copied, Q * k + q)
                    pe.wait_ge(tok2_ready, Q * k + q + 1)
                    for i in range(PK):
                        ins = T.transpose(bank[TURN][:, i * P:(i + 1) * P], pair_of(tok2, k, q, i), w("ident"))
                    ins.then_inc(t2_in_psum, 1)

            def logits():
                small(("logits", 0))
                pe.wait_ge(stats_ready, STATS_AT["logits", 0])
                T.transpose(bank[SMALL][:, 0:P], tile("xsum", P, Q * C), w("ident")).then_inc(small_ready, 1)
                pe.wait_ge(xsum_ready, 1)
                T.matmul(bank[SMALL][:, 0:Q * E], tile("xsumT", P, P), w("wr"), start=True, stop=True).then_inc(logits_in_psum, 1)

            def weights_transposed():
                small(("wt", 0))
                pe.wait_ge(wt_ready, 1)
                T.transpose(bank[SMALL][0:Q * E, 0:P], tile("wsoft", P, Q * E), w("ident")).then_inc(small_ready, 1)

            def weights_spread(q):
                small(("wb", q))
                for e in range(EP):
                    at = (q * EP + e) * P
                    ins = T.matmul(bank[SMALL][:, e * P:(e + 1) * P], r_("sel")[:, at:at + P], tile("wT", Q * E, P), start=True, stop=True)
                ins.then_inc(small_ready, 1)

            def bias_product():
                small(("bias", 0))
                for q in range(Q):
                    ins = T.matmul(bank[SMALL][:, q * P:(q + 1) * P], expert_bias[:, q].rearrange("p h c -> p (h c)"), tile("wT", Q * E, P),
                                   start=True, stop=True)
                ins.then_inc(small_ready, 1)

            def layer1(n):
                k, q, e, h = units[n]
                if n == 0:
                    pe.wait_ge(y_ready, 8)
                    pe.wait_ge(f1_split, 1)
                if n >= 2:
                    pe.wait_ge(h1_ready, n - 1)
                if n % NU == 0:
                    pe.wait_ge(xs_ready, 4 * (k + 1))
                for m, weights in enumerate((f1hi, f1lo)):
                    ins = T.matmul(bank[Z1[n % 2]][:], weights[:, e, :], xs[:, k, q, h::2, :], start=(m == 0), stop=(m == 1))
                ins.then_inc(z1_done, 1)

            def layer2(n):
                e = units[n][2]
                pe.wait_ge(h1_ready, n + 1)
                if n >= 2:
                    if n - 2 < NU:
                        pe.wait_ge(z2_taken, n - 1)
                    else:
                        pe.wait_ge(h2_ready, n - 1 - NU)
                T.matmul(bank[Z2[n % 2]][:], f2s[:, e, :], h1[n % 3][:], start=True, stop=True).then_inc(z2_done, 1)

            def layer3(k, m):
                _, q, e, h = units[k * NU + m]
                src, ready, done = ((held[m], held_ready, mlp_done0), (h2[m % 3][:], h2_ready, mlp_done1))[k]
                pe.wait_ge(ready, m + 1)
                if m == 0 and k == 0:
                    pe.wait_ge(bias_ready, 1)
                    pe.wait_ge(t2_copied, Q * NK)
                T.matmul(bank[OUT[k][q]][h * C:(h + 1) * C, :], wo[:, e, :], src, start=(e == 0), stop=(e == EP - 1)).then_inc(done, 1)

            def unit(n):
                layer1(n)
                if n >= 1:
                    layer2(n - 1)

            stages = {
                "warm": lambda k: warm_up(), "gn1": lambda k: group_product(("gn1", k), w("gn1"), tile(f"gn1v{k}e2", P, 2 * PK), P, 2 * PK),
                "xnorm": conv0, "gn2": lambda k: group_product(("gn2", k), w("gn2"), tile(f"gn2v{k}e2", P, 2 * PK), P, 2 * PK),
                "s2row": lambda k: second_scale_row(), "ebias": lambda k: expert_biases(),
                "conv": lambda u: conv1(u, 0), "convb": lambda u: conv1(u, 1),
                "gn3": lambda k: group_product(("gn3", k), w("gn3"), tile(f"wsum{k}", P, 2 * BK), P, 2 * BK),
                "w2": lambda k: group_product(("w2", k), w("w2", C), tile(f"wmax{k}", C, BK * WIN), C, BK * WIN),
                "gna": lambda k: group_product(("gna", k), w("gna", C), tile(f"wr{k}", C, 2 * BK), C, 2 * BK),
                "w3": lambda k: group_product(("w3", k), w3d[:], tile(f"wan{k}", C, BK * WIN), P, BK * WIN),
                "outp": out_product, "gn4": lambda k: group_product(("gn4", k), w("gn1"), tile(f"gn4v{k}e2", P, 2 * PK), P, 2 * PK),
                "tok": to_tokens, "hch": to_channels, "fc": fc, "score": score, "xt": x_transposes, "t2": residual_transposes,
                "logits": lambda k: logits(), "wt": lambda k: weights_transposed(), "wb": weights_spread,
                "bias": lambda k: bias_product(), "unit": unit,
            }
            for name, k in ORDER:
                if name in stages:
                    stages[name](k)
            for m in range(0, NU + 3):
                if 1 <= m < NU:
                    layer1(NU + m)
                if 1 <= m <= NU:
                    layer2(NU + m - 1)
                if 2 <= m < NU + 2:
                    layer3(1, m - 2)
                if 3 <= m:
                    layer3(0, m - 3)


def lay_out(inp):
    import numpy as np

    f = np.float32
    where, n = columns()
    par = np.zeros((P, n), f)

    def put(name, a):
        a = np.asarray(a)
        a = a.reshape(a.shape[0], -1)
        lo, hi = where[name]
        par[0:a.shape[0], lo:hi] = a

    def twice(a):
        out = np.zeros((2 * a.shape[0], 2 * a.shape[1]), f)
        out[0:a.shape[0], 0:a.shape[1]] = a
        out[a.shape[0]:, a.shape[1]:] = a
        return out

    rows = np.arange(P)
    put("ident", np.eye(P, dtype=f))
    put("ones", np.ones((P, P), f))
    put("gn1", (rows[:, None] // 2 == rows[None, :] // 2) / f(2))
    put("gn2", (rows[:, None] // 4 == rows[None, :] // 4) / f(4))
    group3 = (rows % C) // (C // 2)
    put("gn3", (group3[:, None] == group3[None, :]) / f(C * WIN * 2))
    ch = np.arange(C)
    put("gna", (ch[:, None] // 8 == ch[None, :] // 8) / f(8 * WIN))
    put("w0", twice(inp["L0_conv_w0"][:, :, 0, 0].T))
    put("b0", np.concatenate([inp["L0_conv_b0"]] * 2)[:, None])
    w1 = inp["L0_conv_w1"]
    conv1 = np.zeros((2, C, TAPS, 2, C), f)
    per = w1.shape[1]
    for o in range(2 * C):
        g = o // (2 * C // 4)
        conv1[:, g * per:(g + 1) * per, :, o % 2, o // 2] = w1[o].reshape(per, TAPS)
    radix = lambda v: np.concatenate([v[0::2], v[1::2]])
    put("b1", radix(inp["L0_conv_b1"])[:, None])
    w2 = np.zeros((C, C), f)
    for o in range(C):
        g = o // (C // 2)
        w2[g * (C // 2):(g + 1) * (C // 2), o] = inp["L0_conv_w2"][o, :, 0, 0]
    put("w2", w2)
    put("b2", inp["L0_conv_b2"][:, None])
    w3 = np.zeros((C, 2, 2, C), f)
    b3 = np.zeros((2, C, 2), f)
    for o in range(2 * C):
        g, r, c = o // C, o % 2, o // 2
        w3[g * (C // 2):(g + 1) * (C // 2), 0, r, c] = inp["L0_conv_w3"][o, :, 0, 0]
        w3[g * (C // 2):(g + 1) * (C // 2), 1, 1 - r, c] = inp["L0_conv_w3"][o, :, 0, 0]
        b3[r, c, 0] = inp["L0_conv_b3"][o]
        b3[1 - r, c, 1] = inp["L0_conv_b3"][o]
    put("w3", w3)
    put("b3", b3.reshape(P, 2))
    put("weight", np.concatenate([inp["L0_conv_weight"]] * 2))
    put("fc", twice(inp["L1_attn_fc_w"].T))
    put("fcb", np.concatenate([inp["L1_attn_fc_b"]] * 2)[:, None])
    put("score", twice(inp["L1_attn_score_w"][:, None]))
    put("wr", twice(inp["L1_ffn_Wr"]))
    put("br", np.broadcast_to(inp["L1_ffn_br"], (P, Q, E)))
    both = np.concatenate([inp["L1_ffn_W1"]] * 2, axis=1)
    put("ffn1", both.transpose(1, 0, 2))
    f2 = np.stack([twice(np.zeros((C, C), f))] * EP)
    for e in range(EP):
        f2[e, 0:C, 0:C] = inp["L1_ffn_W2"][2 * e]
        f2[e, C:, C:] = inp["L1_ffn_W2"][2 * e + 1]
    put("ffn2", f2.transpose(1, 0, 2))
    put("ffo", inp["L1_ffn_Wo"].reshape(EP, P, C).transpose(1, 0, 2))
    for i in (1, 2):
        names = [f"L1_ffn_{n}{i}" for n in ("b", "g", "be", "m", "v")]
        put(f"bn{i}", np.stack([inp[n].reshape(EP, P) for n in names]).transpose(2, 0, 1))
    emask = np.zeros((2, HID, EP, Q, E), f)
    row_where, n_rows = columns(ROW_COLS)
    rows_par = np.zeros((Q * E, n_rows), f)
    sel = np.zeros((Q, E, Q, EP, 2, HID), f)
    for e in range(E):
        emask[e % 2, :, e // 2, :, e] = 1
        for q in range(Q):
            sel[q, e, q, e // 2, e % 2, :] = 1
    put("emask", emask.reshape(P, -1))
    bo = np.concatenate([inp["L1_ffn_bo"]] * Q)
    qmask = np.kron(np.eye(Q, dtype=f), np.ones((E, 1), f))
    for name, a in (("sel", sel.reshape(Q * E, -1)), ("bo", bo), ("qmask", qmask)):
        lo, hi = row_where[name]
        rows_par[:, lo:hi] = a
    return par, rows_par, conv1.reshape(P, TAPS, P)


def kernel(**inputs):
    import numpy as np
    import concourse.bacc as bacc
    from concourse.bass_utils import run_bass_kernel_spmd

    inp = {name: np.asarray(a) for name, a in inputs.items()}
    par, rows_par, conv1 = lay_out(inp)
    arrays = {"x": np.ascontiguousarray(inp["x"]), "params": par, "row_params": rows_par, "conv1_w": np.ascontiguousarray(conv1)}
    nc = bacc.Bacc("TRN2", target_bir_lowering=False, num_devices=1)
    aps = [nc.dram_tensor(n, a.shape, F32, kind="ExternalInput").ap() for n, a in arrays.items()]
    out = nc.dram_tensor("out", arrays["x"].shape, F32, kind="ExternalOutput").ap()
    conv_attention_experts(nc, *aps, out)
    r = run_bass_kernel_spmd(nc, [arrays], core_ids=[0])
    return r.results[0]["out"]
```

```python
from contextlib import ExitStack

import concourse.bass as bass
from concourse import mybir

ALU = mybir.AluOpType
ACT = mybir.ActivationFunctionType
F32 = mybir.dt.float32
F32R = mybir.dt.float32r
AX_X = mybir.AxisListType.X

P = 128
B, C, S = 16, 64, 16
PIX = S * S
PAIRS = B // 2
NK = 2
PK = PAIRS // NK
BK = B // NK
PAD = S + 2
TAPS = 9
WARM = 2
WIN = 4
E, HID = 8, 64
EP = E // 2
Q = 2
EPS = 1e-5
BN_EPS = 1e-3
LOWEST = -3.0e38

COLS = dict(
    gn1=P, w0=P, b0=1, gn2=P, b1=1, ident=P, gn3=P, gna=C, w2=C, b2=1, w3=2 * P, b3=2, weight=C,
    fc=P, fcb=1, score=2, wr=Q * E, br=Q * E, ffn1=EP * P, ffn2=EP * P, ffo=EP * C,
    bn1=5 * EP, bn2=5 * EP, ones=P, centre=P,
)
ROW_COLS = dict(sel=Q * EP * P, bo=Q * P)


def columns(cols=COLS):
    at, out = 0, {}
    for name, n in cols.items():
        out[name] = (at, at + n)
        at += n
    return out, at


def conv_attention_experts(nc: bass.Bass, x: bass.AP, params: bass.AP, row_params: bass.AP, conv1_w: bass.AP, out: bass.AP):
    where, n_params = columns()
    row_where, n_rows = columns(ROW_COLS)
    n_early = where["b1"][1]
    x_pairs = x.rearrange("(b h) c y x -> b (h c) (y x)", h=2)
    out_pairs = out.rearrange("(b h) c y x -> b (h c) (y x)", h=2)

    with ExitStack() as ctx:
        def sb(name, shape, dt=F32):
            return ctx.enter_context(nc.sbuf_tensor(name, shape, dt))

        def sem(name):
            return ctx.enter_context(nc.semaphore(name))

        par = sb("par", [P, n_params])

        def w(name, rows=P):
            a, b = where[name]
            return par[0:rows, a:b]

        row_par = sb("row_par", [Q * E, n_rows])

        def r_(name):
            a, b = row_where[name]
            return row_par[:, a:b]

        xin = sb("xin", [P, PAIRS, PIX])
        xnorm = sb("xnorm", [P, PAIRS, PIX])
        act0 = sb("act0", [P, PAIRS, PIX])
        norm0 = sb("norm0", [P, PAIRS, PIX])
        pad = [sb(f"pad{h}", [P, PAIRS, PAD, PAD], F32R) for h in range(2)]
        y = sb("y", [P, B, PIX])
        x1 = sb("x1", [P, PAIRS, PIX])
        more = sb("more", [P, 4, 512])
        square = sb("square", [P, NK, Q, BK, C])
        hn = sb("hn", [P, NK, Q, BK, C])
        ctxs = sb("ctxs", [P, NK, Q, C, BK])
        xs = sb("xs", [P, NK, Q, BK, P], F32R)
        h1 = [sb(f"h1_{i}", [P, 512]) for i in range(3)]

        def by_block(t, pattern, **sizes):
            return t[:].rearrange("p b n -> p (b n)").rearrange(pattern, k=NK, q=Q, **sizes)

        hch = by_block(xnorm, "p (k q n) -> p k q n")
        qch = by_block(act0, "p (k q n) -> p k q n")
        gated = by_block(norm0, "p (k q c t) -> p k q c t", c=C)
        decay = square[:].rearrange("p k q b c -> p (k q b c)").rearrange("p (k q c t) -> p k q c t", k=NK, q=Q, c=C)
        xn2 = hn
        res = act0
        held = [y[:, 2 * i:2 * i + 2, :].rearrange("p b n -> p (b n)") for i in range(8)]
        held += [t[:, 2 * i:2 * i + 2, :].rearrange("p b n -> p (b n)") for t in (xin, xnorm) for i in range(4)]
        held += [more[:, i, :] for i in range(4)]
        held += [norm0[:, 2 * i:2 * i + 2, :].rearrange("p b n -> p (b n)") for i in range(4)]
        held += [t[:, k, q].rearrange("p a b -> p (a b)") for t in (ctxs, square) for k in range(NK) for q in range(Q)]

        w1raw = sb("w1raw", [P, TAPS, P])
        w1hi = sb("w1hi", [P, TAPS, P], F32R)
        w1lo = sb("w1lo", [P, TAPS, P], F32R)
        f1hi = sb("f1hi", [P, EP, P], F32R)
        f1lo = sb("f1lo", [P, EP, P], F32R)
        f2s = sb("f2s", [P, EP, P])
        w3d = sb("w3d", [C, P])
        b3d = sb("b3d", [P, 1])
        b2half = sb("b2half", [C, 1])
        wb = sb("wb", [P, Q, EP, P])
        bias_ch = sb("bias_ch", [P, Q, P])
        minus_half = sb("minus_half", [P, 32])
        warm = sb("warm", [P, 512], mybir.dt.bfloat16)

        small_names = {}

        def tile(name, rows, *dims):
            n = 1
            for d in dims:
                n *= d
            if name not in small_names:
                small_names[name] = sb("s_" + name, [P, n])
            t = small_names[name][0:rows, 0:n]
            if len(dims) == 2:
                return t.rearrange("p (a b) -> p a b", a=dims[0])
            if len(dims) == 3:
                return t.rearrange("p (a b c) -> p a b c", a=dims[0], b=dims[1])
            return t

        bank = [ctx.enter_context(nc.psum_tensor(f"bank{i}", [P, 512], F32)) for i in range(8)]
        CONV0 = ((0, 1), (5, 6))
        CONV1 = (2, 3)
        CHAIN = ((5, 6), (0, 1))
        SMALL = 4
        TURN = 7
        Z1, Z2 = (2, 3), (5, 6)
        OUT = ((0, 7), (1, 4))

        def sem_list(*names):
            return [sem(n) for n in names]

        (early_params_loaded, params_loaded, conv1_w_loaded, rows_loaded, out_stored) = sem_list(
            "early_params_loaded", "params_loaded", "conv1_w_loaded", "rows_loaded", "out_stored")
        x_loaded = [sem(f"x_loaded_{n}") for n in range(PAIRS // 2)]
        vector_done = sem("vector_done")
        pool_done = sem("pool_done")
        small_ready = sem("small_ready")
        small_free = sem("small_free")
        var_ready = sem("var_ready")
        rstd_ready = sem("rstd_ready")
        stats_ready = sem("stats_ready")
        pads_zeroed, consts_ready, warm_ready = sem_list("pads_zeroed", "consts_ready", "warm_ready")
        w1_hi_ready, w1_split, f1_split, weights_folded = sem_list("w1_hi_ready", "w1_split", "f1_split", "weights_folded")
        xnorm_ready, conv0_done, act0_ready, norm0_ready = sem_list("xnorm_ready", "conv0_done", "act0_ready", "norm0_ready")
        pad_hi_ready, pad_lo_ready, conv1_done, y_ready = sem_list("pad_hi_ready", "pad_lo_ready", "conv1_done", "y_ready")
        window_tanh_ready = sem("window_tanh_ready")
        gn3_shift_ready, y_normalised, gated_y_ready = sem_list("gn3_shift_ready", "y_normalised", "gated_y_ready")
        outconv_done, gn4_shift_ready, x_scaled, x1_ready = sem_list("outconv_done", "gn4_shift_ready", "x_scaled", "x1_ready")
        tok_in_psum, square_ready, hn_ready, ctx_ready = sem_list("tok_in_psum", "square_ready", "hn_ready", "ctx_ready")
        hch_in_psum, hch_ready, fc_done, qch_ready = sem_list("hch_in_psum", "hch_ready", "fc_done", "qch_ready")
        exps_in, exps_ready, coef_ready, decay_ready = sem_list("exps_in", "exps_ready", "coef_ready", "decay_ready")
        tok2_ready, centred2, square2_ready, xn2_ready = sem_list("tok2_ready", "centred2", "square2_ready", "xn2_ready")
        xsum_ready = sem("xsum_ready")
        xt_ready = sem("xt_ready")
        xs_hi, xs_ready = sem_list("xs_hi", "xs_ready")
        logits_ready, wexp_ready, wt_ready = sem_list("logits_ready", "wexp_ready", "wt_ready")
        ctx_in_psum, bias_ready, t2_biased = sem_list("ctx_in_psum", "bias_ready", "t2_biased")
        z1_done, h1_ready, z2_done = sem_list("z1_done", "h1_ready", "z2_done")
        h2_ready = sem("h2_ready")
        weighed = sem("weighed")
        mlp_done, res_ready = sem_list("mlp_done", "res_ready")

        ORDER = [(s.split(".")[0], int(s.split(".")[1])) for s in """
            warm.0 warm.1 warm.2 warm.3 warm.4 warm.5 gn1.0 warm.6 warm.7 gn1f.0 xnorm.0 gn1.1 warm.8 gn2.0 warm.9 gn1f.1 silu0.0 warm.10
            warm.11 gn2f.0 warm.12 w1.0 warm.13 xnorm.1 warm.14 warm.15 conv.0 conv.1 norm0.0 silu0.1 silu.0 bn.0 conv.2 low0.0 conv.3 gn2.1
            ws.0 conv.4 gn2f.1 bnf.0 conv.5 conv.6 silu.1 conv.7 conv.8 ws.1 norm0.1 low0.1 conv.9 silu.2 conv.10 ws.2 s2row.0 conv.11
            conv.12 ws.3 warm.16 conv.13 gn3.0 warm.17 warm.18 silu.3 gn3f.0 win.0 conv.14 conv.15 w2.0 conv.16 gna.0 gnaf.0 ws.4 silu.4
            ynorm.0 wan.0 conv.17 warm.19 silu.5 ynorm.1 conv.18 w3.0 ws.5 silu.6 conv.19 conv.20 gate.0 gate.1 outp.0 conv.21 gn4.0 warm.20
            conv.22 warm.21 gn4f.0 conv.23 warm.22 tok.0 ws.6 warm.23 warm.24 warm.25 x1.0 warm.26 ws.7 silu.7 heat.0 heat.1 heat.2 ln1.0
            ln1.1 heat.3 warm.27 hch.0 gn3.1 hn.0 fc.0 gn3f.1 warm.28 hch.1 hn.1 win.1 coef.0 score.0 heat.4 w2.1 fc.1 att.0 warm.29 score.1
            warm.30 gna.1 warm.31 ynorm.2 coef.1 heat.5 gnaf.1 ynorm.3 scan.0 warm.32 warm.33 att.1 wan.1 t2.0 heat.6 w3.1 scan.1 gate.2
            heat.7 heat.8 heat.9 gate.3 ln2.0 t2.1 outp.1 heat.10 heat.11 gn4.1 gn4f.1 xn2.0 ln2.1 x1.1 heat.12 heat.13 xn2.1 xt.0 ln1.2
            heat.14 heat.15 tok.1 xt.1 unit.0 ln1.3 unit.1 unit.2 hch.2 unit.3 hn.2 hch.3 hn.3 fc.2 unit.4 score.2 coef.2 fc.3 att.2 unit.5
            score.3 coef.3 unit.6 unit.7 att.3 scan.2 unit.8 t2.2 scan.3 unit.9 ln2.2 unit.10 unit.11 unit.12 xn2.2 t2.3 xt.2 unit.13 ln2.3
            unit.14 unit.15 unit.16 xn2.3 unit.17 unit.18 sums.0 unit.19 logits.0 unit.20 unit.21 wt.0 xt.3 unit.22 wb.0 unit.23 unit.24
            mix.0 mix.1 mix.2 mix.3 mix.4 unit.25 mix.5 unit.26 mix.6 unit.27 wb.1 mix.7 mix.8 mix.9 bias.0 unit.28 unit.29 unit.30 mix.10
            unit.31 mix.11 mix.12 mix.13 mix.14 mix.15 mix.16 mix.17 mix.18 mix.19 mix.20 mix.21 mix.22 finish.0 mix.23 mix.24 finish.1
            mix.25 unit.32 mix.26 mix.27 finish.2 mix.28 mix.29 mix.30 mix.31 finish.3
        """.split()]

        def positions(names):
            found = [s for s in ORDER if s[0] in names]
            return {s: i + 1 for i, s in enumerate(found)}

        SMALL_AT = positions({"gn1", "gn2", "s2row", "gn3", "w2", "gna", "w3", "gn4", "score", "sums", "logits", "wt", "wb", "bias"})
        STATS_AT = positions({"gn1", "gn2", "gn3", "w2", "gna", "w3", "gn4"})
        var_tiles, VAR_AT, at = {}, {}, 0
        for name, k in ORDER:
            parts = {"gn1f": [("gn1", P, PK)], "gn2f": [("gn2", P, PK)], "gn3f": [("gn3", P, BK)], "gnaf": [("gna", C, BK)],
                     "gn4f": [("gn4", P, PK)], "bn": [("bnv", P, 2 * EP)],
                     "ln1": [("ln1", P, BK)], "ln2": [("ln2", P, BK)]}.get(name, [])
            for part, rows, cols in parts:
                at += 1
                VAR_AT[part, k] = at
                var_tiles[part, k] = (f"{part}v{k}", rows, cols)

        def rstd(name):
            n, rows, cols = var_tiles[name]
            return tile(n + "r", rows, cols)

        def halves(k, q):
            return slice(k * PK, (k + 1) * PK), slice(q * P, (q + 1) * P)

        def image(k, i):
            return bank[CHAIN[k][i // 2]][:, (i % 2) * PIX:(i % 2 + 1) * PIX]

        def tokens(n):
            return bank[CHAIN[n // Q][n % Q]][:].rearrange("p (b c) -> p b c", c=C)

        units = [(k, q, e, h) for k in range(NK) for q in range(Q) for e in range(EP) for h in range(2)]
        NU = len(units)
        mixes = sorted(range(NU), key=lambda n: (units[n][1], units[n][0], n))
        PER_OUT = 2 * EP

        block = ctx.enter_context(nc.Block())

        @block.sync
        def _(sp):
            for n in range(PAIRS // 2):
                pairs = slice(2 * n, 2 * n + 2)
                sp.dma_start(xin[:, pairs, :], x_pairs[pairs].rearrange("b p n -> p b n")).then_inc(x_loaded[n], 16)
            sp.dma_start(w1raw[:], conv1_w).then_inc(conv1_w_loaded, 16)
            sp.dma_start(par[:, n_early:], params[:, n_early:]).then_inc(params_loaded, 16)
            sp.dma_start(row_par[:], row_params).then_inc(rows_loaded, 16)
            for n in range(Q * NK):
                q, k = n // NK, n % NK
                pairs, pixels = halves(k, q)
                sp.wait_ge(res_ready, n + 1)
                sp.dma_start(out_pairs[pairs, :, pixels].rearrange("b p n -> p b n"),
                             res[:, pairs, pixels]).then_inc(out_stored, 16)
            sp.wait_ge(out_stored, 16 * Q * NK)

        @block.gpsimd
        def _(pool):
            G = nc.gpsimd
            steps = [0]

            def step(ins):
                steps[0] += 1
                ins.then_inc(pool_done, 1)
                pool.wait_ge(pool_done, steps[0])

            def power(name):
                n, rows, cols = var_tiles[name]
                pool.wait_ge(var_ready, VAR_AT[name])
                G.tensor_tensor(rstd(name), tile(n, rows, cols), minus_half[0:rows, 0:cols], ALU.pow).then_inc(rstd_ready, 1)

            def split_w1():
                pool.wait_ge(w1_hi_ready, 1)
                G.tensor_tensor(w1lo[:], w1raw[:], w1hi[:].bitcast(F32), ALU.subtract).then_inc(w1_split, 1)

            def sum_samples(n):
                k, q = n // Q, n % Q
                pool.wait_ge(xn2_ready, n + 1)
                t = tile(f"xsum{n}", P, 4, C)
                step(G.tensor_tensor(t, xn2[:, k, q, 0:4, :], xn2[:, k, q, 4:8, :], ALU.add))
                step(G.tensor_tensor(t[:, 0:2, :], t[:, 0:2, :], t[:, 2:4, :], ALU.add))
                step(G.tensor_tensor(t[:, 0, :], t[:, 0, :], t[:, 1, :], ALU.add))
                if k == NK - 1:
                    G.tensor_tensor(tile("xsum", P, Q, C)[:, q, :], tile(f"xsum{q}", P, 4, C)[:, 0, :], t[:, 0, :],
                                    ALU.add).then_inc(xsum_ready, 1)

            def bias_residual():
                pool.wait_ge(bias_ready, 1)
                pool.wait_ge(tok2_ready, Q * NK)
                for n in range(Q * NK):
                    q, k = n // NK, n % NK
                    pairs, pixels = halves(k, q)
                    G.tensor_tensor(x1[:, pairs, pixels], x1[:, pairs, pixels], bias_ch[:, q:q + 1, :].broadcast_to([P, PK, P]),
                                    ALU.add).then_inc(t2_biased, 1)

            G.memset(warm[:], 0.0).then_inc(warm_ready, 1)
            G.memset(minus_half[:], -0.5).then_inc(consts_ready, 1)
            for h in range(2):
                G.memset(pad[h][:].bitcast(F32), 0.0).then_inc(pads_zeroed, 1)
            pool.wait_ge(consts_ready, 1)
            for name, k in ORDER:
                if name == "gn1f":
                    power(("gn1", k))
                elif name == "w1":
                    split_w1()
                elif name == "bn":
                    power(("bnv", k))
                elif name in ("gn2f", "gn3f", "gnaf", "gn4f"):
                    power((name[:-1], k))
                elif name in ("ln1", "ln2"):
                    power((name, k))
                elif name == "xn2":
                    sum_samples(k)
                elif name == "bias":
                    bias_residual()

        @block.scalar
        def _(act):
            A = nc.scalar
            act.dma_start(par[:, 0:n_early], params[:, 0:n_early]).then_inc(early_params_loaded, 16)

            def silu0(k):
                for j in range(2):
                    act.wait_ge(conv0_done, 2 * k + j + 1)
                    b = k * PK + 2 * j
                    A.activation(act0[:, b:b + 2, :], bank[CONV0[k][j]][:].rearrange("p (b n) -> p b n", b=2),
                                 ACT.Silu, bias=w("b0")).then_inc(act0_ready, 1)

            def high_w1():
                act.wait_ge(conv1_w_loaded, 16)
                A.activation(w1hi[:], w1raw[:], ACT.Copy).then_inc(w1_hi_ready, 1)

            def pad_high(k):
                act.wait_ge(pads_zeroed, 2)
                for h in range(2):
                    own = slice(h * C, (h + 1) * C)
                    for j in range(2):
                        act.wait_ge(norm0_ready, 2 * k + j + 1)
                        pairs = slice(k * PK + 2 * j, k * PK + 2 * j + 2)
                        A.activation(pad[h][own, pairs, 1:S + 1, 1:S + 1],
                                     norm0[own, pairs, :].rearrange("p b (y x) -> p b y x", y=S),
                                     ACT.Copy).then_inc(pad_hi_ready, 1)

            def silu1(u):
                act.wait_ge(conv1_done, u + 1)
                k, j, h = u // 4, (u // 2) % 2, u % 2
                b = 2 * (k * PK + 2 * j) + h
                A.activation(y[:, b:b + 3:2, :], bank[CONV1[u % 2]][:].rearrange("p (b n) -> p b n", b=2),
                             ACT.Silu, bias=w("b1")).then_inc(y_ready, 1)

            def window_tanh(k):
                act.wait_ge(small_free, SMALL_AT["w2", k])
                A.activation(tile(f"wth{k}", C, BK * WIN), tile(f"wh{k}", C, BK * WIN), ACT.Tanh).then_inc(window_tanh_ready, 1)

            def normalise_y(n):
                k = n // 2
                act.wait_ge(gn3_shift_ready, k + 1)
                r, nb = rstd(("gn3", k)), tile(f"gn3v{k}nb", P, BK)
                for b in range(n % 2 * PK, n % 2 * PK + PK):
                    img = y[:, k * BK + b, :]
                    A.activation(img, img, ACT.Identity, bias=nb[:, b:b + 1], scale=r[:, b:b + 1]).then_inc(y_normalised, 1)

            def scale_residual(k):
                act.wait_ge(gn4_shift_ready, k + 1)
                r, nb = rstd(("gn4", k)), tile(f"gn4v{k}nb", P, PK)
                for i in range(PK):
                    A.activation(x1[:, k * PK + i, :], image(k, i), ACT.Identity, bias=nb[:, i:i + 1],
                                 scale=r[:, i:i + 1]).then_inc(x_scaled, 1)

            def radix_tanh(k):
                act.wait_ge(small_ready, SMALL_AT["w3", k])
                A.activation(tile(f"wt{k}", P, BK * WIN), bank[SMALL][:, 0:BK * WIN], ACT.Tanh,
                             bias=b3d[:, 0:1], scale=0.5).then_inc(small_free, 1)

            def squares(n):
                act.wait_ge(tok_in_psum, n + 1)
                A.activation(square[:, n // Q, n % Q], tokens(n), ACT.Square).then_inc(square_ready, 1)

            def hch_copies(n):
                act.wait_ge(hch_in_psum, n + 1)
                A.activation(hch[:, n // Q, n % Q, :], bank[CHAIN[n // Q][n % Q]][:], ACT.Copy).then_inc(hch_ready, 1)

            def fc_tanh(n):
                act.wait_ge(fc_done, n + 1)
                A.activation(qch[:, n // Q, n % Q, :], bank[CHAIN[n // Q][n % Q]][:], ACT.Tanh, bias=w("fcb")).then_inc(qch_ready, 1)

            def attention_exps(n):
                act.wait_ge(exps_in, n + 1)
                A.activation(tile(f"aexp{n}", P, 2 * BK), tile(f"aarg{n}", P, 2 * BK), ACT.Exp).then_inc(exps_ready, 1)

            def spread_decay(n):
                act.wait_ge(coef_ready, n + 1)
                A.activation(decay[:, n // Q, n % Q], tile(f"ascan{n}", P, BK).rearrange("p (o b) -> p o b", o=1).broadcast_to([P, C, BK]),
                             ACT.Copy).then_inc(decay_ready, 1)

            def squares2(n):
                act.wait_ge(centred2, n + 1)
                A.activation(square[:, n // Q, n % Q], tokens(n), ACT.Square).then_inc(square2_ready, 1)

            def high_x(n):
                act.wait_ge(xt_ready, n + 1)
                k, q = n // Q, n % Q
                for h in range(2):
                    own = slice(h * C, (h + 1) * C)
                    A.activation(xs[own, k, q, h::2, :], bank[CHAIN[k][q]][own, :].rearrange("p (b n) -> p b n", b=PK),
                                 ACT.Copy).then_inc(xs_hi, 1)

            def relu1(n):
                act.wait_ge(z1_done, n + 1)
                if n >= 3:
                    act.wait_ge(z2_done, n - 2)
                e = units[n][2]
                A.activation(h1[n % 3][:], bank[Z1[n % 2]][:], ACT.Relu, bias=tile("bnb", P, 2 * EP)[:, e:e + 1],
                             scale=tile("bns", P, 2 * EP)[:, e:e + 1]).then_inc(h1_ready, 1)

            def relu2(n):
                act.wait_ge(z2_done, n + 1)
                e = units[n][2]
                A.activation(held[n], bank[Z2[n % 2]][:], ACT.Relu,
                             bias=tile("bnb", P, 2 * EP)[:, EP + e:EP + e + 1]).then_inc(h2_ready, 1)

            def route():
                act.wait_ge(logits_ready, 1)
                A.activation(tile("wexp", P, Q * E), tile("lg", P, Q * E), ACT.Exp).then_inc(wexp_ready, 1)

            def weights_copy(q):
                act.wait_ge(small_ready, SMALL_AT["wb", q])
                A.activation(wb[:, q], bank[SMALL][:].rearrange("p (e n) -> p e n", e=EP), ACT.Copy).then_inc(small_free, 1)

            def unit(n):
                if n < NU:
                    relu1(n)
                if n >= 1:
                    relu2(n - 1)

            stages = {"silu0": silu0, "norm0": pad_high, "silu": silu1, "w2": window_tanh, "ynorm": normalise_y,
                      "x1": scale_residual, "w3": radix_tanh, "ln1": squares, "hch": hch_copies, "fc": fc_tanh, "coef": attention_exps, "att": spread_decay, "ln2": squares2,
                      "xt": high_x, "unit": unit, "wb": weights_copy,
                      "w1": lambda k: high_w1()}
            act.wait_ge(early_params_loaded, 16)
            for name, k in ORDER:
                if name in stages:
                    stages[name](k)
                elif name == "logits":
                    route()

        @block.vector
        def _(dve):
            steps = [0]

            def step(ins):
                steps[0] += 1
                ins.then_inc(vector_done, 1)
                dve.wait_ge(vector_done, steps[0])

            V = nc.vector

            def each(t, rows, n, width):
                return t.rearrange("p (b o) -> p b o", o=1).broadcast_to([rows, n, width])

            def group_finish(name, n, rows=P):
                t, _, _ = var_tiles[name]
                ms, sq = tile(t + "ms", rows, 2, n), tile(t + "sq", rows, n)
                dve.wait_ge(small_ready, SMALL_AT[name])
                V.tensor_copy(ms, bank[SMALL][0:rows, 0:2 * n].rearrange("p (a n) -> p a n", a=2)).then_inc(small_free, 1)
                dve.wait_ge(small_free, SMALL_AT[name])
                step(V.tensor_tensor(sq, ms[:, 0, :], ms[:, 0, :], ALU.mult))
                V.scalar_tensor_tensor(tile(t, rows, n), ms[:, 1, :], EPS, sq, ALU.add, ALU.subtract).then_inc(var_ready, 1)

            def group_shift(name, n, rows=P, signal=None):
                t, _, _ = var_tiles[name]
                dve.wait_ge(rstd_ready, VAR_AT[name])
                ins = V.scalar_tensor_tensor(tile(t + "nb", rows, n), tile(t + "ms", rows, 2, n)[:, 0, :], -1.0, rstd(name),
                                             ALU.mult, ALU.mult)
                if signal is None:
                    step(ins)
                else:
                    ins.then_inc(signal, 1)
                    dve.wait_ge(signal, name[1] + 1)
                return rstd(name), tile(t + "nb", rows, n)

            def channel_stats(name, source, n, arrived=None):
                t, _, _ = var_tiles[name]
                raw, mv, e2 = tile(t + "raw", P, n, 6), tile(t + "mv", P, n, 2), tile(t + "e2", P, 2, n)
                for i in range(n):
                    if arrived is not None:
                        arrived(i)
                    ins = V.bn_stats(raw[:, i, :], source(i))
                step(ins)
                for i in range(n):
                    ins = V.bn_aggr(mv[:, i, :], raw[:, i, :])
                step(ins)
                V.tensor_copy(e2[:, 0, :], mv[:, :, 0])
                step(V.tensor_tensor(e2[:, 1, :], mv[:, :, 0], mv[:, :, 0], ALU.mult))
                V.tensor_tensor(e2[:, 1, :], e2[:, 1, :], mv[:, :, 1], ALU.add).then_inc(stats_ready, 1)

            def gn1_stats(k):
                channel_stats(("gn1", k), lambda i: xin[:, k * PK + i, :], PK,
                              lambda i: dve.wait_ge(x_loaded[(k * PK + i) // 2], 16))

            def normalise_x(k):
                r, nb = group_shift(("gn1", k), PK)
                for i in range(PK):
                    V.tensor_scalar(xnorm[:, k * PK + i, :], xin[:, k * PK + i, :], r[:, i:i + 1], nb[:, i:i + 1],
                                    ALU.mult, ALU.add).then_inc(xnorm_ready, 1)

            def gn2_stats(k):
                channel_stats(("gn2", k), lambda i: act0[:, k * PK + i, :], PK,
                              lambda i: dve.wait_ge(act0_ready, 2 * k + i // 2 + 1))

            def normalise_0(k):
                r, nb = group_shift(("gn2", k), PK)
                for i in range(PK):
                    ins = V.tensor_scalar(norm0[:, k * PK + i, :], act0[:, k * PK + i, :], r[:, i:i + 1], nb[:, i:i + 1],
                                          ALU.mult, ALU.add)
                    if i % 2:
                        ins.then_inc(norm0_ready, 1)

            def low_0(k):
                dve.wait_ge(norm0_ready, 2 * k + 2)
                for h in range(2):
                    own, other = slice(h * C, (h + 1) * C), slice((1 - h) * C, (2 - h) * C)
                    for j in range(2):
                        dve.wait_ge(pad_hi_ready, 4 * k + 2 * h + j + 1)
                        pairs = slice(k * PK + 2 * j, k * PK + 2 * j + 2)
                        V.tensor_tensor(pad[h][other, pairs, 1:S + 1, 1:S + 1],
                                        norm0[own, pairs, :].rearrange("p b (y x) -> p b y x", y=S),
                                        pad[h][own, pairs, 1:S + 1, 1:S + 1].bitcast(F32), ALU.subtract).then_inc(pad_lo_ready, 1)

            def batch_norm_variances():
                dve.wait_ge(params_loaded, 16)
                bn1, bn2 = (w(n).rearrange("p (a e) -> p a e", a=5) for n in ("bn1", "bn2"))
                bnvar = tile("bnvv0", P, 2 * EP)
                V.tensor_scalar(bnvar[:, 0:EP], bn1[:, 4, :], BN_EPS, None, ALU.add)
                V.tensor_scalar(bnvar[:, EP:2 * EP], bn2[:, 4, :], BN_EPS, None, ALU.add).then_inc(var_ready, 1)

            def fold_weights():
                bn1, bn2 = (w(n).rearrange("p (a e) -> p a e", a=5) for n in ("bn1", "bn2"))
                bns, bnb = tile("bns", P, 2 * EP), tile("bnb", P, 2 * EP)
                dve.wait_ge(rstd_ready, VAR_AT["bnv", 0])
                r = rstd(("bnv", 0))
                V.tensor_tensor(bns[:, 0:EP], bn1[:, 1, :], r[:, 0:EP], ALU.mult)
                V.tensor_tensor(bns[:, EP:2 * EP], bn2[:, 1, :], r[:, EP:2 * EP], ALU.mult)
                V.tensor_tensor(bnb[:, 0:EP], bn1[:, 0, :], bn1[:, 3, :], ALU.subtract)
                step(V.tensor_tensor(bnb[:, EP:2 * EP], bn2[:, 0, :], bn2[:, 3, :], ALU.subtract))
                step(V.tensor_tensor(bnb, bnb, bns, ALU.mult))
                V.tensor_tensor(bnb[:, 0:EP], bnb[:, 0:EP], bn1[:, 2, :], ALU.add)
                step(V.tensor_tensor(bnb[:, EP:2 * EP], bnb[:, EP:2 * EP], bn2[:, 2, :], ALU.add))
                diag = tile("diag", P, EP, P)
                for e in range(EP):
                    V.tensor_scalar(diag[:, e, :], w("ident"), bns[:, EP + e:EP + e + 1], None, ALU.mult)
                V.tensor_scalar(b2half[:], w("b2", C), 0.5, None, ALU.mult)
                V.tensor_tensor(w3d[:], w("w3", C)[:, 0:P], w("w3", C)[:, P:2 * P], ALU.subtract)
                step(V.tensor_tensor(b3d[:], w("b3")[:, 0:1], w("b3")[:, 1:2], ALU.subtract))
                V.tensor_scalar(b3d[:], b3d[:], 0.5, None, ALU.mult).then_inc(weights_folded, 1)

            def scale_second_layer():
                dve.wait_ge(small_ready, SMALL_AT["s2row", 0])
                V.tensor_tensor(f2s[:], w("ffn2").rearrange("p (e m) -> p e m", e=EP),
                                bank[SMALL][:].rearrange("p (e m) -> p e m", e=EP), ALU.mult).then_inc(small_free, 1)
                f1 = w("ffn1").rearrange("p (e m) -> p e m", e=EP)
                step(V.tensor_copy(f1hi[:], f1))
                V.tensor_tensor(f1lo[:], f1, f1hi[:].bitcast(F32), ALU.subtract).then_inc(f1_split, 1)

            def window_stats(u):
                dve.wait_ge(y_ready, u + 1)
                k, j, h = u // 4, (u // 2) % 2, u % 2
                ws = tile(f"ws{k}", P, BK * WIN, 6)
                for i in range(2):
                    b = 2 * (2 * j + i) + h
                    img = y[:, k * BK + b, :].rearrange("p (a y c x) -> p a y c x", a=2, y=8, c=2)
                    for n in range(WIN):
                        ins = V.bn_stats(ws[:, b * WIN + n, :], img[:, n // 2, :, n % 2, :])
                step(ins)

            def gn3_stats(k):
                n = BK * WIN
                ws = tile(f"ws{k}", P, n, 6)
                st, sq, sm = tile(f"wst{k}", P, 2, n), tile(f"wsq{k}", P, n, 2), tile(f"wsm{k}", P, 2, n)
                means = ws.rearrange("p n (a t) -> p n a t", a=2)[:, :, :, 1]
                V.tensor_tensor(sq, means, means, ALU.mult)
                V.tensor_tensor(st[:, 0, :], ws[:, :, 1], ws[:, :, 4], ALU.add)
                step(V.tensor_tensor(sm[:, 0, :], ws[:, :, 2], ws[:, :, 5], ALU.add))
                step(V.tensor_tensor(sm[:, 1, :], sq[:, :, 0], sq[:, :, 1], ALU.add))
                step(V.scalar_tensor_tensor(st[:, 1, :], sm[:, 0, :], 1.0 / 32, sm[:, 1, :], ALU.mult, ALU.add))
                V.tensor_reduce(tile(f"wsum{k}", P, 2 * BK), st.rearrange("p a (b n) -> p (a b) n", n=WIN), AX_X,
                                ALU.add).then_inc(stats_ready, 1)

            def window_in(k):
                r, nb = group_shift(("gn3", k), BK, signal=gn3_shift_ready)
                st = tile(f"wst{k}", P, 2, BK * WIN)
                a = tile(f"win{k}", P, BK, WIN)
                step(V.scalar_tensor_tensor(a, st[:, 0, :].rearrange("p (b n) -> p b n", n=WIN), 0.5, each(r, P, BK, WIN),
                                            ALU.mult, ALU.mult))
                step(V.tensor_tensor(a, a, each(nb, P, BK, WIN), ALU.add))
                other = tile(f"wino{k}", C, BK, WIN)
                step(V.tensor_copy(other, a[C:P]))
                V.tensor_tensor(tile(f"wmax{k}", C, BK, WIN), a[0:C], other, ALU.max).then_inc(stats_ready, 1)

            def window_half(k):
                dve.wait_ge(small_ready, SMALL_AT["w2", k])
                V.tensor_scalar(tile(f"wh{k}", C, BK * WIN), bank[SMALL][0:C, 0:BK * WIN], 0.5, b2half[:, 0:1],
                                ALU.mult, ALU.add).then_inc(small_free, 1)

            def window_norm_stats(k):
                wa = tile(f"wa{k}", C, 2, BK * WIN)
                dve.wait_ge(window_tanh_ready, k + 1)
                step(V.scalar_tensor_tensor(wa[:, 0, :], tile(f"wth{k}", C, BK * WIN), 1.0, tile(f"wh{k}", C, BK * WIN),
                                            ALU.add, ALU.mult))
                step(V.tensor_tensor(wa[:, 1, :], wa[:, 0, :], wa[:, 0, :], ALU.mult))
                V.tensor_reduce(tile(f"wr{k}", C, 2 * BK), wa.rearrange("p a (b n) -> p (a b) n", n=WIN), AX_X,
                                ALU.add).then_inc(stats_ready, 1)

            def window_normalise(k):
                r, nb = group_shift(("gna", k), BK, C)
                a = tile(f"wa{k}", C, 2, BK * WIN)[:, 0, :].rearrange("p (b n) -> p b n", n=WIN)
                an = tile(f"wan{k}", C, BK, WIN)
                step(V.tensor_tensor(an, a, each(r, C, BK, WIN), ALU.mult))
                V.tensor_tensor(an, an, each(nb, C, BK, WIN), ALU.add).then_inc(stats_ready, 1)

            def gate_y(n):
                k, j = n // 2, n % 2
                g = tile(f"gate{k}", P, BK * 2, S)
                if j == 0:
                    dve.wait_ge(small_free, SMALL_AT["w3", k])
                    step(V.tensor_scalar(g.rearrange("p n (c x) -> p (n c) x", c=2), each(tile(f"wt{k}", P, BK * WIN), P, BK * WIN, 8),
                                         0.5, 0.5, ALU.mult, ALU.add))
                dve.wait_ge(y_normalised, BK * k + 4 * j + 4)
                yk = y[:, k * BK + 4 * j:k * BK + 4 * j + 4, :].rearrange("p b (a y x) -> p (b a) y x", a=2, y=8)
                gj = g[:, 8 * j:8 * j + 8, :]
                V.tensor_tensor(yk, yk, gj.rearrange("p n (o x) -> p n o x", o=1).broadcast_to([P, BK, 8, S]),
                                ALU.mult).then_inc(gated_y_ready, 1)

            def gn4_stats(k):
                channel_stats(("gn4", k), lambda i: image(k, i), PK, lambda i: dve.wait_ge(outconv_done, 2 * k + i // 2 + 1))

            def residual1(k):
                group_shift(("gn4", k), PK, signal=gn4_shift_ready)
                for i in range(PK):
                    dve.wait_ge(x_scaled, PK * k + i + 1)
                    V.tensor_tensor(x1[:, k * PK + i, :], x1[:, k * PK + i, :], xin[:, k * PK + i, :], ALU.add).then_inc(x1_ready, 1)

            def layer_norm_stats(name, n):
                dve.wait_ge(square_ready if name == "ln1" else square2_ready, n + 1)
                sq = tile(f"{name}sq{n}", P, BK)
                step(V.tensor_reduce(sq, square[:, n // Q, n % Q], AX_X, ALU.add))
                V.tensor_scalar(tile(var_tiles[name, n][0], P, BK), sq, 1.0 / C, EPS, ALU.mult, ALU.add).then_inc(var_ready, 1)

            def layer_norm_scale(name, n, ready):
                dve.wait_ge(rstd_ready, VAR_AT[name, n])
                V.tensor_tensor(hn[:, n // Q, n % Q], tokens(n), each(rstd((name, n)), P, BK, C), ALU.mult).then_inc(ready, 1)

            runmax, runsum = tile("runmax", P, Q, B + 1), tile("runsum", P, Q, B + 1)

            def attention_coefficients(n):
                k, q = n // Q, n % Q
                t0, t1 = k * BK, (k + 1) * BK
                e, top = tile(f"scores{n}", P, BK), runmax[:, q]
                dve.wait_ge(small_ready, SMALL_AT["score", n])
                if k == 0:
                    V.memset(top[:, 0:1], LOWEST)
                    V.memset(runsum[:, q, 0:1], 0.0)
                V.tensor_copy(e, bank[SMALL][:, 0:BK]).then_inc(small_free, 1)
                dve.wait_ge(small_free, SMALL_AT["score", n])
                step(V.tensor_tensor_scan(top[:, t0 + 1:t1 + 1], e, e, top[:, t0:t0 + 1], ALU.max, ALU.max))
                arg = tile(f"aarg{n}", P, 2, BK)
                V.tensor_tensor(arg[:, 0], top[:, t0:t1], top[:, t0 + 1:t1 + 1], ALU.subtract)
                V.tensor_tensor(arg[:, 1], e, top[:, t0 + 1:t1 + 1], ALU.subtract).then_inc(exps_in, 1)

            def attend(n):
                k, q = n // Q, n % Q
                t0, t1 = k * BK, (k + 1) * BK
                dve.wait_ge(exps_ready, n + 1)
                ex, total = tile(f"aexp{n}", P, 2, BK), runsum[:, q]
                inv, b_, a_, ascan = (tile(f"{part}{n}", P, BK) for part in ("inv", "coefb", "coefa", "ascan"))
                V.memset(ascan[:, 0:1], 0.0)
                step(V.tensor_tensor_scan(total[:, t0 + 1:t1 + 1], ex[:, 0, :], ex[:, 1, :], total[:, t0:t0 + 1], ALU.mult, ALU.add))
                V.tensor_tensor(a_, ex[:, 0], total[:, t0:t1], ALU.mult)
                step(V.reciprocal(inv, total[:, t0 + 1:t1 + 1]))
                V.tensor_tensor(b_, ex[:, 1], inv, ALU.mult)
                step(V.tensor_tensor(a_, a_, inv, ALU.mult))
                V.tensor_copy(ascan[:, 1:], a_[:, 1:]).then_inc(coef_ready, 1)
                step(V.tensor_tensor(gated[:, k, q], hn[:, k, q].rearrange("p b c -> p c b"),
                                     b_.rearrange("p (o b) -> p o b", o=1).broadcast_to([P, C, BK]), ALU.mult))
                if k:
                    dve.wait_ge(ctx_ready, q + 1)
                    step(V.scalar_tensor_tensor(gated[:, k, q, :, 0], ctxs[:, k - 1, q, :, BK - 1], a_[:, 0:1],
                                                gated[:, k, q, :, 0], ALU.mult, ALU.add))

            def scan_context(n):
                k, q = n // Q, n % Q
                flat = lambda t: t[:, k, q].rearrange("p c b -> p (c b)")
                dve.wait_ge(decay_ready, n + 1)
                V.tensor_tensor_scan(flat(ctxs), flat(decay), flat(gated), 0.0, ALU.mult, ALU.add).then_inc(ctx_ready, 1)

            def residual2(n):
                pairs, pixels = halves(n // Q, n % Q)
                dve.wait_ge(ctx_in_psum, n + 1)
                V.tensor_tensor(x1[:, pairs, pixels], x1[:, pairs, pixels], bank[TURN][:].rearrange("p (b n) -> p b n", b=PK),
                                ALU.add).then_inc(tok2_ready, 1)

            def low_x(n):
                k, q = n // Q, n % Q
                dve.wait_ge(xs_hi, 2 * n + 2)
                for h in range(2):
                    own, other = slice(h * C, (h + 1) * C), slice((1 - h) * C, (2 - h) * C)
                    V.tensor_tensor(xs[other, k, q, h::2, :], bank[CHAIN[k][q]][own, :].rearrange("p (b n) -> p b n", b=PK),
                                    xs[own, k, q, h::2, :].bitcast(F32), ALU.subtract).then_inc(xs_ready, 1)

            def turned_sum():
                dve.wait_ge(small_ready, SMALL_AT["sums", 0])
                V.tensor_copy(tile("xsumT", P, P), bank[SMALL][:, 0:P]).then_inc(small_free, 1)

            def routing_weights():
                dve.wait_ge(small_ready, SMALL_AT["logits", 0])
                lg, mx = tile("lg", P, Q, E), tile("lmax", P, Q)
                V.scalar_tensor_tensor(lg, bank[SMALL][:, 0:Q * E].rearrange("p (q e) -> p q e", q=Q), 1.0 / B,
                                       w("br").rearrange("p (q e) -> p q e", q=Q), ALU.mult, ALU.add).then_inc(small_free, 1)
                dve.wait_ge(small_free, SMALL_AT["logits", 0])
                step(V.tensor_reduce(mx, lg, AX_X, ALU.max))
                V.tensor_tensor(lg, lg, each(mx, P, Q, E), ALU.subtract).then_inc(logits_ready, 1)
                ex, sm = tile("wexp", P, Q, E), tile("wsum", P, Q)
                dve.wait_ge(wexp_ready, 1)
                step(V.tensor_reduce(sm, ex, AX_X, ALU.add))
                step(V.reciprocal(sm, sm))
                V.tensor_tensor(tile("wsoft", P, Q, E), ex, each(sm, P, Q, E), ALU.mult).then_inc(wt_ready, 1)

            def weights_turned():
                dve.wait_ge(small_ready, SMALL_AT["wt", 0])
                V.tensor_copy(tile("wT", Q * E, P), bank[SMALL][0:Q * E, 0:P]).then_inc(small_free, 1)

            def bias_taken():
                dve.wait_ge(small_ready, SMALL_AT["bias", 0])
                V.tensor_copy(bias_ch[:], bank[SMALL][:, 0:Q * P].rearrange("p (q n) -> p q n", q=Q)).then_inc(bias_ready, 1)

            def weigh(m):
                n = mixes[m]
                _, q, e, _ = units[n]
                dve.wait_ge(small_free, SMALL_AT["wb", q])
                dve.wait_ge(h2_ready, n + 1)
                t = held[n].rearrange("p (b n) -> p b n", b=PK)
                V.tensor_tensor(t, t, wb[:, q, e:e + 1, :].broadcast_to([P, PK, P]), ALU.mult).then_inc(weighed, 1)

            def finish(n):
                q, k = n // NK, n % NK
                dve.wait_ge(mlp_done, PER_OUT * (n + 1))
                dve.wait_ge(t2_biased, n + 1)
                pairs, pixels = halves(k, q)
                V.tensor_tensor(res[:, pairs, pixels], bank[OUT[k][q]][:].rearrange("p (b n) -> p b n", b=PK),
                                x1[:, pairs, pixels], ALU.add).then_inc(res_ready, 1)

            stages = {
                "gn1": gn1_stats, "gn1f": lambda k: group_finish(("gn1", k), PK), "xnorm": normalise_x,
                "gn2": gn2_stats, "gn2f": lambda k: group_finish(("gn2", k), PK), "norm0": normalise_0, "low0": low_0,
                "bn": lambda k: batch_norm_variances(), "bnf": lambda k: fold_weights(),
                "s2row": lambda k: scale_second_layer(),
                "ws": window_stats, "gn3": gn3_stats, "gn3f": lambda k: group_finish(("gn3", k), BK), "win": window_in,
                "w2": window_half, "gna": window_norm_stats, "gnaf": lambda k: group_finish(("gna", k), BK, C),
                "wan": window_normalise, "gate": gate_y, "gn4": gn4_stats, "gn4f": lambda k: group_finish(("gn4", k), PK),
                "x1": residual1, "ln1": lambda n: layer_norm_stats("ln1", n), "hn": lambda k: layer_norm_scale("ln1", k, hn_ready),
                "coef": attention_coefficients, "att": attend, "scan": scan_context, "ln2": lambda n: layer_norm_stats("ln2", n), "t2": residual2,
                "xn2": lambda k: layer_norm_scale("ln2", k, xn2_ready), "xt": low_x, "sums": lambda k: turned_sum(),
                "logits": lambda k: routing_weights(), "mix": weigh, "finish": finish,
                "wt": lambda k: weights_turned(), "bias": lambda k: bias_taken(),
            }
            for name, k in ORDER:
                if name in stages:
                    stages[name](k)

        @block.tensor
        def _(pe):
            T = nc.tensor

            def small(name):
                if SMALL_AT[name] > 1:
                    pe.wait_ge(small_free, SMALL_AT[name] - 1)

            def group_product(name, matrix, rhs, rows, n):
                small(name)
                pe.wait_ge(stats_ready, STATS_AT[name])
                T.matmul(bank[SMALL][0:rows, 0:n], matrix, rhs, start=True, stop=True).then_inc(small_ready, 1)

            def warm_up(n):
                for _ in range(WARM):
                    T.matmul(bank[TURN][:], warm[:, 0:P], warm[:], start=True, stop=True)

            def keep_warm(n):
                if n == 0:
                    pe.wait_ge(y_ready, 8)
                for _ in range(WARM):
                    T.matmul(bank[Z1[0]][:], warm[:, 0:P], warm[:], start=True, stop=True)

            def conv0(k):
                for j in range(PK // 2):
                    b = k * PK + 2 * j
                    pe.wait_ge(xnorm_ready, b + 2)
                    T.matmul(bank[CONV0[k][j]][:], w("w0"), xnorm[:, b:b + 2, :], start=True, stop=True).then_inc(conv0_done, 1)

            def second_scale_row():
                small(("s2row", 0))
                pe.wait_ge(params_loaded, 16)
                pe.wait_ge(weights_folded, 1)
                T.matmul(bank[SMALL][:], w("ones"), tile("diag", P, EP * P), start=True, stop=True).then_inc(small_ready, 1)

            wo = w("ffo").rearrange("p (e m) -> p e m", e=EP)

            def conv1(n):
                u, dy = n // 3, n % 3
                k, j, h = u // 4, (u // 2) % 2, u % 2
                if dy == 0:
                    if u == 0:
                        pe.wait_ge(w1_split, 1)
                    pe.wait_ge(pad_lo_ready, 4 * k + 2 * h + j + 1)
                    if u >= 2:
                        pe.wait_ge(y_ready, u - 1)
                b = k * PK + 2 * j
                for dx in range(3):
                    for weights in (w1hi, w1lo):
                        ins = T.matmul(bank[CONV1[u % 2]][:], weights[:, 3 * dy + dx, :], pad[h][:, b:b + 2, dy:dy + S, dx:dx + S],
                                       start=(dy == dx == 0 and weights is w1hi), stop=(dy == dx == 2 and weights is w1lo))
                if dy == 2:
                    ins.then_inc(conv1_done, 1)

            def out_product(k):
                if k == 0:
                    pe.wait_ge(act0_ready, 4)
                for j in range(2):
                    pe.wait_ge(gated_y_ready, 2 * k + j + 1)
                    b = k * BK + 4 * j
                    for h in range(2):
                        ins = T.matmul(bank[CHAIN[k][j]][h * C:(h + 1) * C, :], w("weight"), y[:, b + h:b + h + 3:2, :], start=True, stop=True)
                    ins.then_inc(outconv_done, 1)

            def centre(k, q, i):
                return T.matmul(bank[CHAIN[k][q]][:, i * P:(i + 1) * P], x1[:, k * PK + i, q * P:(q + 1) * P], w("centre"),
                                start=True, stop=True)

            def to_tokens(k):
                pe.wait_ge(x_scaled, PK * (k + 1))
                for i in range(PK):
                    pe.wait_ge(x1_ready, PK * k + i + 1)
                    for q in range(Q):
                        ins = centre(k, q, i)
                        if i == PK - 1:
                            ins.then_inc(tok_in_psum, 1)

            def pair_of(t, k, q, i):
                return t[:, k, q, 2 * i:2 * i + 2, :].rearrange("p b c -> p (b c)")

            def to_channels(n):
                k, q = n // Q, n % Q
                pe.wait_ge(hn_ready, n + 1)
                for i in range(PK):
                    ins = T.transpose(bank[CHAIN[k][q]][:, i * P:(i + 1) * P], pair_of(hn, k, q, i), w("ident"))
                ins.then_inc(hch_in_psum, 1)

            def fc(n):
                k, q = n // Q, n % Q
                pe.wait_ge(hch_ready, n + 1)
                T.matmul(bank[CHAIN[k][q]][:], w("fc"), hch[:, k, q, :], start=True, stop=True).then_inc(fc_done, 1)

            def score(n):
                k, q = n // Q, n % Q
                small(("score", n))
                pe.wait_ge(qch_ready, n + 1)
                for i in range(PK):
                    ins = T.matmul(bank[SMALL][:, 2 * i:2 * i + 2], qch[:, k, q, i * P:(i + 1) * P], w("score"), start=True, stop=True)
                ins.then_inc(small_ready, 1)

            def x_transposes(n):
                k, q = n // Q, n % Q
                pe.wait_ge(xn2_ready, n + 1)
                for i in range(PK):
                    ins = T.transpose(bank[CHAIN[k][q]][:, i * P:(i + 1) * P], pair_of(xn2, k, q, i), w("ident"))
                ins.then_inc(xt_ready, 1)

            def context_transposes(n):
                k, q = n // Q, n % Q
                if n:
                    pe.wait_ge(tok2_ready, n)
                pe.wait_ge(ctx_ready, n + 1)
                for i in range(PK):
                    for h in range(2):
                        ins = T.matmul(bank[TURN][h * C:(h + 1) * C, i * P:(i + 1) * P], ctxs[:, k, q, :, 2 * i + h], w("ident"),
                                       start=True, stop=True)
                ins.then_inc(ctx_in_psum, 1)

            def centre_again(n):
                k, q = n // Q, n % Q
                pe.wait_ge(qch_ready, n + 1)
                pe.wait_ge(tok2_ready, n + 1)
                for i in range(PK):
                    ins = centre(k, q, i)
                ins.then_inc(centred2, 1)

            def turn_sums():
                small(("sums", 0))
                pe.wait_ge(xsum_ready, Q)
                T.transpose(bank[SMALL][:, 0:P], tile("xsum", P, Q * C), w("ident")).then_inc(small_ready, 1)

            def logits():
                small(("logits", 0))
                T.matmul(bank[SMALL][:, 0:Q * E], tile("xsumT", P, P), w("wr"), start=True, stop=True).then_inc(small_ready, 1)

            def weights_transposed():
                small(("wt", 0))
                pe.wait_ge(wt_ready, 1)
                T.transpose(bank[SMALL][0:Q * E, 0:P], tile("wsoft", P, Q * E), w("ident")).then_inc(small_ready, 1)

            def weights_spread(q):
                small(("wb", q))
                pe.wait_ge(rows_loaded, 16)
                for e in range(EP):
                    at = (q * EP + e) * P
                    ins = T.matmul(bank[SMALL][:, e * P:(e + 1) * P], r_("sel")[:, at:at + P], tile("wT", Q * E, P), start=True, stop=True)
                ins.then_inc(small_ready, 1)

            def bias_product():
                small(("bias", 0))
                for q in range(Q):
                    ins = T.matmul(bank[SMALL][:, q * P:(q + 1) * P], r_("bo")[:, q * P:(q + 1) * P], tile("wT", Q * E, P),
                                   start=True, stop=True)
                ins.then_inc(small_ready, 1)

            def layer1(n):
                k, q, e, h = units[n]
                if n == 0:
                    pe.wait_ge(y_ready, 8)
                    pe.wait_ge(f1_split, 1)
                if n >= 2:
                    pe.wait_ge(h1_ready, n - 1)
                pe.wait_ge(xs_ready, 4 * k + 2 * (q + 1))
                for m, weights in enumerate((f1hi, f1lo)):
                    ins = T.matmul(bank[Z1[n % 2]][:], weights[:, e, :], xs[:, k, q, h::2, :], start=(m == 0), stop=(m == 1))
                ins.then_inc(z1_done, 1)

            def layer2(n):
                e = units[n][2]
                pe.wait_ge(h1_ready, n + 1)
                if n < 2:
                    pe.wait_ge(xs_ready, 2 * n + 2)
                else:
                    pe.wait_ge(h2_ready, n - 1)
                T.matmul(bank[Z2[n % 2]][:], f2s[:, e, :], h1[n % 3][:], start=True, stop=True).then_inc(z2_done, 1)

            def layer3(m):
                k, q, e, h = units[mixes[m]]
                pe.wait_ge(weighed, m + 1)
                if m % PER_OUT == 0:
                    last, count = {0: (xs_ready, 4 * NK), 7: (tok2_ready, Q * NK), 1: (xs_ready, 4 * NK), 4: (bias_ready, 1)}[OUT[k][q]]
                    pe.wait_ge(last, count)
                T.matmul(bank[OUT[k][q]][h * C:(h + 1) * C, :], wo[:, e, :], held[mixes[m]], start=(e == 0), stop=(e == EP - 1)).then_inc(mlp_done, 1)

            def unit(n):
                if n < NU:
                    layer1(n)
                if n >= 1:
                    layer2(n - 1)

            stages = {
                "warm": warm_up, "heat": keep_warm, "gn1": lambda k: group_product(("gn1", k), w("gn1"), tile(f"gn1v{k}e2", P, 2 * PK), P, 2 * PK),
                "xnorm": conv0, "gn2": lambda k: group_product(("gn2", k), w("gn2"), tile(f"gn2v{k}e2", P, 2 * PK), P, 2 * PK),
                "s2row": lambda k: second_scale_row(),
                "conv": conv1,
                "gn3": lambda k: group_product(("gn3", k), w("gn3"), tile(f"wsum{k}", P, 2 * BK), P, 2 * BK),
                "w2": lambda k: group_product(("w2", k), w("w2", C), tile(f"wmax{k}", C, BK * WIN), C, BK * WIN),
                "gna": lambda k: group_product(("gna", k), w("gna", C), tile(f"wr{k}", C, 2 * BK), C, 2 * BK),
                "w3": lambda k: group_product(("w3", k), w3d[:], tile(f"wan{k}", C, BK * WIN), P, BK * WIN),
                "outp": out_product, "gn4": lambda k: group_product(("gn4", k), w("gn1"), tile(f"gn4v{k}e2", P, 2 * PK), P, 2 * PK),
                "tok": to_tokens, "hch": to_channels, "fc": fc, "score": score, "xt": x_transposes, "t2": context_transposes, "ln2": centre_again,
                "sums": lambda k: turn_sums(), "logits": lambda k: logits(), "mix": layer3, "wt": lambda k: weights_transposed(), "wb": weights_spread,
                "bias": lambda k: bias_product(), "unit": unit,
            }
            pe.wait_ge(warm_ready, 1)
            for name, k in ORDER:
                if (name, k) == ("gn1", 0):
                    pe.wait_ge(early_params_loaded, 16)
                if name in stages:
                    stages[name](k)


def lay_out(inp):
    import numpy as np

    f = np.float32
    where, n = columns()
    par = np.zeros((P, n), f)

    def put(name, a):
        a = np.asarray(a)
        a = a.reshape(a.shape[0], -1)
        lo, hi = where[name]
        par[0:a.shape[0], lo:hi] = a

    def twice(a):
        out = np.zeros((2 * a.shape[0], 2 * a.shape[1]), f)
        out[0:a.shape[0], 0:a.shape[1]] = a
        out[a.shape[0]:, a.shape[1]:] = a
        return out

    rows = np.arange(P)
    put("ident", np.eye(P, dtype=f))
    put("ones", np.ones((P, P), f))
    put("centre", np.eye(P, dtype=f) - (rows[:, None] // C == rows[None, :] // C) / f(C))
    put("gn1", (rows[:, None] // 2 == rows[None, :] // 2) / f(2))
    put("gn2", (rows[:, None] // 4 == rows[None, :] // 4) / f(4))
    group3 = (rows % C) // (C // 2)
    put("gn3", (group3[:, None] == group3[None, :]) / f(C * WIN * 2))
    ch = np.arange(C)
    put("gna", (ch[:, None] // 8 == ch[None, :] // 8) / f(8 * WIN))
    put("w0", twice(inp["L0_conv_w0"][:, :, 0, 0].T))
    put("b0", np.concatenate([inp["L0_conv_b0"]] * 2)[:, None])
    w1 = inp["L0_conv_w1"]
    conv1 = np.zeros((2, C, TAPS, 2, C), f)
    per = w1.shape[1]
    for o in range(2 * C):
        g = o // (2 * C // 4)
        conv1[:, g * per:(g + 1) * per, :, o % 2, o // 2] = w1[o].reshape(per, TAPS)
    radix = lambda v: np.concatenate([v[0::2], v[1::2]])
    put("b1", radix(inp["L0_conv_b1"])[:, None])
    w2 = np.zeros((C, C), f)
    for o in range(C):
        g = o // (C // 2)
        w2[g * (C // 2):(g + 1) * (C // 2), o] = inp["L0_conv_w2"][o, :, 0, 0]
    put("w2", w2)
    put("b2", inp["L0_conv_b2"][:, None])
    w3 = np.zeros((C, 2, 2, C), f)
    b3 = np.zeros((2, C, 2), f)
    for o in range(2 * C):
        g, r, c = o // C, o % 2, o // 2
        w3[g * (C // 2):(g + 1) * (C // 2), 0, r, c] = inp["L0_conv_w3"][o, :, 0, 0]
        w3[g * (C // 2):(g + 1) * (C // 2), 1, 1 - r, c] = inp["L0_conv_w3"][o, :, 0, 0]
        b3[r, c, 0] = inp["L0_conv_b3"][o]
        b3[1 - r, c, 1] = inp["L0_conv_b3"][o]
    put("w3", w3)
    put("b3", b3.reshape(P, 2))
    put("weight", np.concatenate([inp["L0_conv_weight"]] * 2))
    put("fc", twice(inp["L1_attn_fc_w"].T))
    put("fcb", np.concatenate([inp["L1_attn_fc_b"]] * 2)[:, None])
    put("score", twice(inp["L1_attn_score_w"][:, None]))
    put("wr", twice(inp["L1_ffn_Wr"]))
    put("br", np.broadcast_to(inp["L1_ffn_br"], (P, Q, E)))
    both = np.concatenate([inp["L1_ffn_W1"]] * 2, axis=1)
    put("ffn1", both.transpose(1, 0, 2))
    f2 = np.stack([twice(np.zeros((C, C), f))] * EP)
    for e in range(EP):
        f2[e, 0:C, 0:C] = inp["L1_ffn_W2"][2 * e]
        f2[e, C:, C:] = inp["L1_ffn_W2"][2 * e + 1]
    put("ffn2", f2.transpose(1, 0, 2))
    put("ffo", inp["L1_ffn_Wo"].reshape(EP, P, C).transpose(1, 0, 2))
    for i in (1, 2):
        names = [f"L1_ffn_{n}{i}" for n in ("b", "g", "be", "m", "v")]
        put(f"bn{i}", np.stack([inp[n].reshape(EP, P) for n in names]).transpose(2, 0, 1))
    row_where, n_rows = columns(ROW_COLS)
    rows_par = np.zeros((Q * E, n_rows), f)
    sel = np.zeros((Q, E, Q, EP, 2, HID), f)
    for e in range(E):
        for q in range(Q):
            sel[q, e, q, e // 2, e % 2, :] = 1
    bo = twice(np.concatenate([inp["L1_ffn_bo"]] * 2, axis=1))
    for name, a in (("sel", sel.reshape(Q * E, -1)), ("bo", bo)):
        lo, hi = row_where[name]
        rows_par[:, lo:hi] = a
    return par, rows_par, conv1.reshape(P, TAPS, P)


def kernel(**inputs):
    import numpy as np
    import concourse.bacc as bacc
    from concourse.bass_utils import run_bass_kernel_spmd

    inp = {name: np.asarray(a) for name, a in inputs.items()}
    par, rows_par, conv1 = lay_out(inp)
    arrays = {"x": np.ascontiguousarray(inp["x"]), "params": par, "row_params": rows_par, "conv1_w": np.ascontiguousarray(conv1)}
    nc = bacc.Bacc("TRN2", target_bir_lowering=False, num_devices=1)
    aps = [nc.dram_tensor(n, a.shape, F32, kind="ExternalInput").ap() for n, a in arrays.items()]
    out = nc.dram_tensor("out", arrays["x"].shape, F32, kind="ExternalOutput").ap()
    conv_attention_experts(nc, *aps, out)
    r = run_bass_kernel_spmd(nc, [arrays], core_ids=[0])
    return r.results[0]["out"]
```
